# Optimizing a Trainium2 kernel written in Bass

```python
import numpy as np
import jax
import jax.numpy as jnp

def _softmax(x, axis=-1):
    return jax.nn.softmax(x, axis=axis)

def _gelu(x):
    return jax.nn.gelu(x, approximate=True)

def _silu(x):
    return jax.nn.silu(x)

def _sigmoid(x):
    return jax.nn.sigmoid(x)

def _layernorm(x, axis=-1, eps=1e-05):
    m = jnp.mean(x, axis=axis, keepdims=True)
    v = jnp.var(x, axis=axis, keepdims=True)
    return (x - m) / jnp.sqrt(v + eps)

def _scatter_add(tgt, idx, src, axis=0):
    return tgt.at[idx].add(src)

def _segment_sum(src, seg, n):
    return jax.ops.segment_sum(src, seg, n)
kernel_name = 'mk_adj_preln_d4_adj_r2_c4ac04'

def setup_inputs(seed: int=0):
    np.random.seed(seed)
    _w = jnp.asarray

    def _rec_inputs():
        import jax
        import jax.numpy as jnp
        _gk = jax.random.key(seed)
        x = -0.0002928 + 1 * jax.random.normal(jax.random.fold_in(_gk, 1), (64, 128, 256), jnp.float32)
        _w = (1.0 + jnp.arange(128, dtype=jnp.float32)) ** (-0.5)
        _w = _w / _w.mean()
        _pij = jnp.clip(0.0625 * _w[:, None] * _w[None, :], 0.0, 1.0)
        _a = jax.random.uniform(jax.random.fold_in(_gk, 2), (128, 128)) < _pij
        adj = _a.astype(jnp.int32)
        return (x, adj)
    x, adj = _rec_inputs()

    def _L0_gnn_setup():
        import jax, jax.numpy as jnp
        import numpy as np
        D_MODEL = 256
        NUM_HEADS = 8
        D_HEAD = D_MODEL // NUM_HEADS
        B, N = (4, 1024)
        key = jax.random.key(seed)
        ks = jax.random.split(key, 10)
        s = 1.0 / np.sqrt(D_MODEL)
        inp = {'h': jax.random.normal(ks[0], (B, N, D_MODEL), dtype=jnp.float32), 'adj': jax.random.randint(ks[1], (N, N), 0, 2, dtype=jnp.int32), 'Wq': jax.random.uniform(ks[2], (D_MODEL, D_MODEL), jnp.float32, -s, s), 'bq': jax.random.uniform(ks[3], (D_MODEL,), jnp.float32, -s, s), 'Wk': jax.random.uniform(ks[4], (D_MODEL, D_MODEL), jnp.float32, -s, s), 'bk': jax.random.uniform(ks[5], (D_MODEL,), jnp.float32, -s, s), 'Wv': jax.random.uniform(ks[6], (D_MODEL, D_MODEL), jnp.float32, -s, s), 'bv': jax.random.uniform(ks[7], (D_MODEL,), jnp.float32, -s, s), 'Wo': jax.random.uniform(ks[8], (D_MODEL, D_MODEL), jnp.float32, -s, s), 'bo': jax.random.uniform(ks[9], (D_MODEL,), jnp.float32, -s, s)}
        return inp
    _L0_gnn_all = _L0_gnn_setup()
    _L0_gnn_in = {k: v for k, v in _L0_gnn_all.items() if k in ('Wq', 'bq', 'Wk', 'bk', 'Wv', 'bv', 'Wo', 'bo')}
    del _L0_gnn_all

    def _L1_gnn_setup():
        import jax, jax.numpy as jnp
        import numpy as np
        B, K, DIN, DOUT = (32, 64, 256, 256)
        key = jax.random.key(seed)
        k1, k2, k3, k4 = jax.random.split(key, 4)
        x = jax.random.normal(k1, (B, K, DIN), dtype=jnp.float32)
        adj = jax.random.randint(k2, (K, K), 0, 2, dtype=jnp.int32)
        W = jax.random.normal(k3, (DOUT, 2 * DIN), dtype=jnp.float32) * 0.02
        b = jax.random.normal(k4, (DOUT,), dtype=jnp.float32) * 0.02
        return {'x': x, 'adj': adj, 'W': W, 'b': b}
    _L1_gnn_all = _L1_gnn_setup()
    _L1_gnn_in = {k: v for k, v in _L1_gnn_all.items() if k in ('W', 'b')}
    del _L1_gnn_all

    def _L2_gnn_setup():
        import jax, jax.numpy as jnp
        import numpy as np
        LEAKY_ALPHA = 0.01
        NEG_INF = -1000000000.0
        LN_EPS = 1e-05

        def _gat_heads(x, adj, W, a):
            O = W.shape[-1]
            Wh = jnp.einsum('bnf,hfo->bhno', x, W)
            f1 = jnp.einsum('bhno,ho->bhn', Wh, a[:, :O])
            f2 = jnp.einsum('bhno,ho->bhn', Wh, a[:, O:])
            e = f1[:, :, :, None] + f2[:, :, None, :]
            e = jnp.where(e > 0, e, LEAKY_ALPHA * e)
            e = jnp.where(adj[None, None] > 0, e, NEG_INF)
            attn = jax.nn.softmax(e, axis=-1)
            return jnp.einsum('bhnm,bhmo->bhno', attn, Wh)
        key = jax.random.key(seed)
        ks = jax.random.split(key, 10)
        B, N, F_in, F_hid, H, F_out, D_ff = (8, 1024, 256, 256, 4, 256, 256)
        s = 0.05
        return {'enc_inputs': jax.random.normal(ks[0], (B, N, F_in), jnp.float32), 'adj': jax.random.randint(ks[1], (N, N), 0, 2, jnp.int32), 'W_heads': jax.random.normal(ks[2], (H, F_in, F_hid), jnp.float32) * s, 'a_heads': jax.random.normal(ks[3], (H, 2 * F_hid), jnp.float32) * s, 'W_out': jax.random.normal(ks[4], (H * F_hid, F_out), jnp.float32) * s, 'a_out': jax.random.normal(ks[5], (2 * F_out,), jnp.float32) * s, 'w1': jax.random.normal(ks[6], (F_out, D_ff), jnp.float32) * s, 'b1': jnp.zeros((D_ff,), jnp.float32), 'w2': jax.random.normal(ks[7], (D_ff, F_out), jnp.float32) * s, 'b2': jnp.zeros((F_out,), jnp.float32), 'ln_gamma': jnp.ones((F_out,), jnp.float32), 'ln_beta': jnp.zeros((F_out,), jnp.float32)}
    _L2_gnn_all = _L2_gnn_setup()
    _L2_gnn_in = {k: v for k, v in _L2_gnn_all.items() if k in ('W_heads', 'a_heads', 'W_out', 'a_out', 'w1', 'b1', 'w2', 'b2', 'ln_gamma', 'ln_beta')}
    del _L2_gnn_all

    def _L3_gnn_setup():
        import jax, jax.numpy as jnp
        import numpy as np
        B, N, F, F1 = (512, 75, 256, 128)
        NEG = -1000000000.0
        ALPHA = 0.2
        key = jax.random.key(seed)
        k1, k2, k3, k4 = jax.random.split(key, 4)
        X = jax.random.normal(k1, (B, N, F), dtype=jnp.float32)
        A = jax.random.randint(k2, (N, N), 0, 2, dtype=jnp.int32)
        W = jax.random.normal(k3, (F, F1), dtype=jnp.float32) * (1.0 / np.sqrt(F))
        a = jax.random.normal(k4, (2, F1, 1), dtype=jnp.float32) * (1.0 / np.sqrt(F1))
        return {'X': X, 'A': A, 'W': W, 'a': a}
    _L3_gnn_all = _L3_gnn_setup()
    _L3_gnn_in = {k: v for k, v in _L3_gnn_all.items() if k in ('W', 'a')}
    del _L3_gnn_all
    return {'x': x, 'adj': adj, 'L0_gnn_Wq': _L0_gnn_in['Wq'], 'L0_gnn_bq': _L0_gnn_in['bq'], 'L0_gnn_Wk': _L0_gnn_in['Wk'], 'L0_gnn_bk': _L0_gnn_in['bk'], 'L0_gnn_Wv': _L0_gnn_in['Wv'], 'L0_gnn_bv': _L0_gnn_in['bv'], 'L0_gnn_Wo': _L0_gnn_in['Wo'], 'L0_gnn_bo': _L0_gnn_in['bo'], 'L1_gnn_W': _L1_gnn_in['W'], 'L1_gnn_b': _L1_gnn_in['b'], 'L2_gnn_W_heads': _L2_gnn_in['W_heads'], 'L2_gnn_a_heads': _L2_gnn_in['a_heads'], 'L2_gnn_W_out': _L2_gnn_in['W_out'], 'L2_gnn_a_out': _L2_gnn_in['a_out'], 'L2_gnn_w1': _L2_gnn_in['w1'], 'L2_gnn_b1': _L2_gnn_in['b1'], 'L2_gnn_w2': _L2_gnn_in['w2'], 'L2_gnn_b2': _L2_gnn_in['b2'], 'L2_gnn_ln_gamma': _L2_gnn_in['ln_gamma'], 'L2_gnn_ln_beta': _L2_gnn_in['ln_beta'], 'L3_gnn_W': _L3_gnn_in['W'], 'L3_gnn_a': _L3_gnn_in['a']}

def reference(x, adj, L0_gnn_Wq, L0_gnn_bq, L0_gnn_Wk, L0_gnn_bk, L0_gnn_Wv, L0_gnn_bv, L0_gnn_Wo, L0_gnn_bo, L1_gnn_W, L1_gnn_b, L2_gnn_W_heads, L2_gnn_a_heads, L2_gnn_W_out, L2_gnn_a_out, L2_gnn_w1, L2_gnn_b1, L2_gnn_w2, L2_gnn_b2, L2_gnn_ln_gamma, L2_gnn_ln_beta, L3_gnn_W, L3_gnn_a):
    import jax
    import jax.numpy as jnp

    def _L0_gnn_ref(h, adj, Wq, bq, Wk, bk, Wv, bv, Wo, bo):
        import jax, jax.numpy as jnp
        import numpy as np
        D_MODEL = 256
        NUM_HEADS = 8
        D_HEAD = D_MODEL // NUM_HEADS
        B, N = (4, 1024)
        b, n, _ = h.shape

        def split_heads(x):
            return x.reshape(b, n, NUM_HEADS, D_HEAD).transpose(0, 2, 1, 3)
        q = split_heads(h @ Wq.T + bq)
        k = split_heads(h @ Wk.T + bk)
        v = split_heads(h @ Wv.T + bv)
        scale = 1.0 / np.sqrt(D_HEAD)
        scores = jnp.einsum('bhqd,bhkd->bhqk', q, k) * scale
        mask = (adj == 0)[None, None, :, :]
        scores = jnp.where(mask, -jnp.inf, scores)
        attn = jax.nn.softmax(scores, axis=-1)
        out = jnp.einsum('bhqk,bhkd->bhqd', attn, v)
        out = out.transpose(0, 2, 1, 3).reshape(b, n, D_MODEL)
        return out @ Wo.T + bo

    def _L1_gnn_ref(x, adj, W, b):
        import jax, jax.numpy as jnp
        import numpy as np
        B, K, DIN, DOUT = (32, 64, 256, 256)
        Din = x.shape[-1]
        Wi, Wj = (W[:, :Din], W[:, Din:])
        mi = jnp.einsum('bkd,od->bko', x, Wi)
        mj = jnp.einsum('bkd,od->bko', x, Wj)
        a = adj.astype(x.dtype)
        deg = a.sum(axis=1)
        out = deg[None, :, None] * (mi + b) + jnp.einsum('ij,bjo->bio', a, mj)
        return out

    def _L2_gnn_ref(enc_inputs, adj, W_heads, a_heads, W_out, a_out, w1, b1, w2, b2, ln_gamma, ln_beta):
        import jax, jax.numpy as jnp
        import numpy as np
        LEAKY_ALPHA = 0.01
        NEG_INF = -1000000000.0
        LN_EPS = 1e-05

        def _gat_heads(x, adj, W, a):
            O = W.shape[-1]
            Wh = jnp.einsum('bnf,hfo->bhno', x, W)
            f1 = jnp.einsum('bhno,ho->bhn', Wh, a[:, :O])
            f2 = jnp.einsum('bhno,ho->bhn', Wh, a[:, O:])
            e = f1[:, :, :, None] + f2[:, :, None, :]
            e = jnp.where(e > 0, e, LEAKY_ALPHA * e)
            e = jnp.where(adj[None, None] > 0, e, NEG_INF)
            attn = jax.nn.softmax(e, axis=-1)
            return jnp.einsum('bhnm,bhmo->bhno', attn, Wh)
        B, N, _ = enc_inputs.shape
        h = jax.nn.elu(_gat_heads(enc_inputs, adj, W_heads, a_heads))
        h = jnp.transpose(h, (0, 2, 1, 3)).reshape(B, N, -1)
        out = _gat_heads(h, adj, W_out[None], a_out[None])[:, 0]
        out = jax.nn.elu(out)
        ffn = jnp.maximum(out @ w1 + b1, 0.0) @ w2 + b2
        y = ffn + out
        mu = jnp.mean(y, axis=-1, keepdims=True)
        var = jnp.var(y, axis=-1, keepdims=True)
        return (y - mu) / jnp.sqrt(var + LN_EPS) * ln_gamma + ln_beta

    def _L3_gnn_ref(X, A, W, a):
        import jax, jax.numpy as jnp
        import numpy as np
        B, N, F, F1 = (512, 75, 256, 128)
        NEG = -1000000000.0
        ALPHA = 0.2
        h = jnp.einsum('bnf,fo->bno', X, W)
        att_self = jnp.einsum('bno,od->bnd', h, a[0])
        att_neigh = jnp.einsum('bno,od->bnd', h, a[1])
        e = att_self + jnp.swapaxes(att_neigh, 1, 2)
        e = jax.nn.leaky_relu(e, ALPHA)
        adj = A.astype(h.dtype)
        e = e + NEG * (1.0 - adj)[None, :, :]
        alpha = jax.nn.softmax(e, axis=-1)
        out = jnp.einsum('bij,bjo->bio', alpha, h)
        return jnp.concatenate([out, h], axis=-1)
    h = jnp.maximum(_layernorm(x, axis=-1), 0.0)
    x = x + _L0_gnn_ref(h, adj, L0_gnn_Wq, L0_gnn_bq, L0_gnn_Wk, L0_gnn_bk, L0_gnn_Wv, L0_gnn_bv, L0_gnn_Wo, L0_gnn_bo)
    h = jnp.maximum(_layernorm(x, axis=-1), 0.0)
    x = x + _L1_gnn_ref(h, adj, L1_gnn_W, L1_gnn_b)
    h = jnp.maximum(_layernorm(x, axis=-1), 0.0)
    x = x + _L2_gnn_ref(h, adj, L2_gnn_W_heads, L2_gnn_a_heads, L2_gnn_W_out, L2_gnn_a_out, L2_gnn_w1, L2_gnn_b1, L2_gnn_w2, L2_gnn_b2, L2_gnn_ln_gamma, L2_gnn_ln_beta)
    h = jnp.maximum(_layernorm(x, axis=-1), 0.0)
    x = x + _L3_gnn_ref(h, adj, L3_gnn_W, L3_gnn_a)
    return x

_drawn_inputs = setup_inputs


def setup_inputs(seed=0):
    import zlib

    import numpy as np

    out = dict(_drawn_inputs(seed))
    spreads = {'L2_gnn_b1': (0.0, 0.278),
     'L2_gnn_b2': (0.0, 0.1),
     'L2_gnn_ln_gamma': (1.0, 0.2),
     'L2_gnn_ln_beta': (0.0, 0.1)}
    factors = {'L0_gnn_Wq': 8.0,
     'L0_gnn_bq': 8.0,
     'L0_gnn_Wk': 8.0,
     'L0_gnn_bk': 8.0,
     'L0_gnn_bv': 2.716,
     'L2_gnn_a_heads': 5.153,
     'L2_gnn_a_out': 6.536,
     'L3_gnn_a': 4.387}
    for name, (base, spread) in spreads.items():
        noise = np.random.default_rng([zlib.crc32(name.encode()), seed]).standard_normal(out[name].shape)
        drawn = base * np.exp(spread * noise) if base else spread * noise
        out[name] = jnp.asarray(drawn.astype(out[name].dtype))
    for name, factor in factors.items():
        out[name] = (out[name] * factor).astype(out[name].dtype)
    return out
```

```python
import numpy as np
import concourse.bass as bass
from concourse import mybir
from contextlib import ExitStack

FP32 = mybir.dt.float32
BF16 = mybir.dt.bfloat16
INT32 = mybir.dt.int32
ALU = mybir.AluOpType
ACT = mybir.ActivationFunctionType
AX = mybir.AxisListType

N = 128
D = 256
KC = D // N
G = 2
H0, DH = 8, 32
H2 = 4
F3 = 128
LN_EPS = 1e-5
LEAK2, LEAK3 = 0.01, 0.2
NEG = -1e9
HIDE = -3e38
PHASES = 4
LAGS = 4


class Step:

    def __init__(self, t, phase, groups):
        self.t, self.phase, self.groups = t, phase, groups

    def group(self, lag):
        g = self.t - lag
        there = not isinstance(g, int) or 0 <= g < self.groups
        return there, g, (self.phase - lag) % 2

    def quarter(self, lag):
        return (self.phase - lag) % 4


def run_steps(eng, groups, step, turn=2):
    for t in range(-2, LAGS):
        step(Step(t, t % turn, groups))
    with eng.Fori(LAGS // turn, (groups - 2) // turn) as i:
        for u in range(turn):
            step(Step(i * turn + u, u, groups))
    for t in range((groups - 2) // turn * turn, groups + LAGS - 1):
        step(Step(t, t % turn, groups))


def positive(n):
    return not isinstance(n, int) or n > 0


def build_program(nc, x, adj, L0_gnn_Wq, L0_gnn_bq, L0_gnn_Wk, L0_gnn_bk, L0_gnn_Wv, L0_gnn_bv, L0_gnn_Wo,
                  L0_gnn_bo, L1_gnn_W, L1_gnn_b, L2_gnn_W_heads, L2_gnn_a_heads, L2_gnn_W_out, L2_gnn_a_out,
                  L2_gnn_w1, L2_gnn_b1, L2_gnn_w2, L2_gnn_b2, L2_gnn_ln_gamma, L2_gnn_ln_beta, L3_gnn_W,
                  L3_gnn_a, shape_consts, out):
    B = x.shape[0]
    NG = B // G
    GD = G * D
    x_d = x.rearrange("b n d -> n b d")
    out_d = out.rearrange("b n d -> n b d")

    ctx = ExitStack()
    with ctx:
        def sb(name, shape, dt=FP32):
            return ctx.enter_context(nc.sbuf_tensor(name, shape, dt))

        def sem(name):
            return ctx.enter_context(nc.semaphore(name))

        x_all = sb("x_all", [N, B, D])
        wqT = sb("wqT", [N, KC, D])
        wkT = sb("wkT", [N, KC, D])
        wvT = sb("wvT", [N, KC, D])
        woT = sb("woT", [N, KC, D])
        w1T = sb("w1T", [N, 2 * KC, D])
        wh = sb("wh", [N, KC, H2, D])
        wh_f = sb("wh_f", [N, KC, DH])
        wout = sb("wout", [N, H2 * KC, D + 2])
        ffn1 = sb("ffn1", [N, KC, D])
        ffn2 = sb("ffn2", [N, KC, D])
        w3 = sb("w3", [N, KC, F3 + 2])
        consts = sb("consts", [N, N + 4 + H2 * N])
        ident = consts[:, 0:N]
        left_mul, left_add = consts[:, N:N + 1], consts[:, N + 1:N + 2]
        right_mul, right_add = consts[:, N + 2:N + 3], consts[:, N + 3:N + 4]
        head_rows = consts[:, N + 4:].rearrange("p (h n) -> p h n", h=H2)
        ident_bf = sb("ident_bf", [N, N], BF16)
        ones = sb("ones", [N, N])
        adj_i = sb("adj_i", [N, N], INT32)
        adj_f = sb("adj_f", [N, N])
        adjT = sb("adjT", [N, N])
        hide0 = sb("hide0", [N, 4, N], BF16)
        hide2 = sb("hide2", [N, 4, N], BF16)
        neg3 = sb("neg3", [N, N])
        edge = sb("edge", [N, N])
        deg = sb("deg", [N, 1])
        edges = sb("edges", [N, 1])
        poison = sb("poison", [N, 1])
        bq_c = sb("bq_c", [N, KC])
        bk_c = sb("bk_c", [N, KC])
        bv_c = sb("bv_c", [N, KC])
        b1_c = sb("b1_c", [N, KC])
        bv_wide = sb("bv_wide", [N, KC, N])
        bo_row = sb("bo_row", [N, 1, D])
        degb_row = sb("degb_row", [N, 1, D])
        b2_row = sb("b2_row", [N, 1, D])
        gamma_row = sb("gamma_row", [N, 1, D])
        beta_row = sb("beta_row", [N, 1, D])
        pow_half = sb("pow_half", [N, G])
        eps_tile = sb("eps_tile", [N, G])
        minus_one = sb("minus_one", [N, G])

        st = sb("st", [N, 2, G, 6])
        mv = sb("mv", [N, 2, G, 2])
        var_eps = sb("var_eps", [N, 2, G])
        rstd = sb("rstd", [N, 2, G])
        mean_rstd = sb("mean_rstd", [N, 2, G])
        shift = sb("shift", [N, 2, G])
        h = sb("h", [N, 2, G, D])
        hT = sb("hT", [N, KC, G, N])

        probs = sb("probs", [N, 4, 4, N])
        probsT = sb("probsT", [N, 4, 4, N])
        qT = sb("qT", [N, KC, G, N])
        kT = sb("kT", [N, KC, G, N])
        v1 = sb("v1", [N, 2, G, H0, DH + 1])
        top0 = sb("top0", [N, 4, 4])
        rsum0 = sb("rsum0", [N, G, H0])
        att0 = sb("att0", [N, G, H0, DH])
        att0T = sb("att0T", [N, KC, G, N])
        hd = sb("hd", [N, 2, G, D])
        hdT = sb("hdT", [N, 2, KC, G, N])
        ahT = sb("ahT", [N, 2, KC, G, N])

        left = sb("left", [64, N])
        right_rows = sb("right_rows", [64, N])
        right = sb("right", [64, H2, N])
        top2 = sb("top2", [N, G, H2])
        sum2 = sb("sum2", [N, G, H2])
        rsum2 = sb("rsum2", [N, G, H2])
        aggT = sb("aggT", [N, KC, H2, G, N])
        em = sb("em", [N, 2, KC, GD // 2])
        headsT = sb("headsT", [N, H2, KC, G, N])
        wh2 = sb("wh2", [N, G, D + 2])
        diag = sb("diag", [N, 2, G, N])
        t3 = sb("t3", [N, 2, G, N])
        negtop = sb("negtop", [N, G])
        sum3 = sb("sum3", [N, 2, G])
        rsum3 = sb("rsum3", [N, G])
        p3T = sb("p3T", [N, G, N])
        em3 = sb("em3", [N, KC, G, N])
        outT = sb("outT", [N, KC, G, N])
        uT = sb("uT", [N, KC, G, N])
        y = sb("y", [N, 2, G, D])
        st_y = sb("st_y", [N, G, 6])
        mv_y = sb("mv_y", [N, 2, G, 2])
        var_y = sb("var_y", [N, G])
        rstd_y = sb("rstd_y", [N, 2, G])
        h3 = sb("h3", [N, 4, G, F3 + 2])

        bank = [ctx.enter_context(nc.psum_tensor(f"bank{i}", [N, 512], FP32)) for i in range(8)]
        raw = probsT[:, :, :, :].rearrange("p a b n -> p (a b n)").rearrange("p (w c d) -> p w c d", w=4, c=2)
        raw1 = y[:, :, :, :].rearrange("p c g d -> p c (g d)")
        a_heads_rows = aggT[:, :, :, :, :].rearrange("p a b c n -> p (a b c n)")
        a_out_rows = em[:, 0, :, :].rearrange("p c n -> p (c n)")[:, 0:2 * D].rearrange("p (s d) -> p s d", s=2)
        a3_rows = h3[:, 0, :, 0:F3]
        prod = headsT[:, :, :, :, :].rearrange("p a b c n -> p (a b c n)")

        loads_done = sem("loads_done")
        later_loads_done = sem("later_loads_done")
        x_loaded = [sem("x_loaded0"), sem("x_loaded1")]
        pool_setup = sem("pool_setup")
        dve_setup = sem("dve_setup")
        weights_T = sem("weights_T")
        weights_dve = sem("weights_dve")
        weights_act = sem("weights_act")
        late_setup = sem("late_setup")
        out_stored = sem("out_stored")

        class Pre:
            def __init__(self, k):
                self.stats = sem(f"stats{k}")
                self.norm = sem(f"norm{k}")
                self.h = sem(f"h{k}")
                self.bias = sem(f"bias{k}")
                self.x = sem(f"x_done{k}")

        pre = [Pre(k) for k in range(4)]

        def pre_dve(dve, k, at):
            there, g, p = at.group(-2)
            if not there:
                return
            s = pre[k]
            if k == 0:
                dve.wait_ge(x_loaded[p], (g - p) * 8 + 16)
            for c in range(G):
                last = nc.vector.bn_stats(st[:, p, c, :], x_all[:, bass.ds(g * G + c, 1), :].rearrange("p a d -> p (a d)"))
            last.then_inc(s.stats, 1)

        def stats_written(dve, k, at):
            there, g, p = at.group(-2)
            if there:
                dve.wait_ge(pre[k].stats, g * 2 + 1)

        def moments_dve(k, at):
            there, g, p = at.group(-2)
            if not there:
                return
            s = pre[k]
            for c in range(G):
                last = nc.vector.bn_aggr(mv[:, p, c, :], st[:, p, c, :])
            last.then_inc(s.stats, 1)

        def pre_pool(pool, k, at):
            there, g, p = at.group(-2)
            if not there:
                return
            s = pre[k]
            pool.wait_ge(s.stats, g * 2 + 2)
            if positive(g - 1):
                pool.wait_ge(s.h, g - 1)
            nc.gpsimd.tensor_tensor(var_eps[:, p, :], mv[:, p, :, 1], eps_tile[:, :], ALU.add).then_inc(s.norm, 1)
            pool.wait_ge(s.norm, g * 4 + 1)
            nc.gpsimd.tensor_tensor(rstd[:, p, :], var_eps[:, p, :], pow_half[:, :], ALU.pow).then_inc(s.norm, 1)
            pool.wait_ge(s.norm, g * 4 + 2)
            nc.gpsimd.tensor_tensor(mean_rstd[:, p, :], mv[:, p, :, 0], rstd[:, p, :], ALU.mult).then_inc(s.norm, 1)
            pool.wait_ge(s.norm, g * 4 + 3)
            nc.gpsimd.tensor_tensor(shift[:, p, :], mean_rstd[:, p, :], minus_one[:, :], ALU.mult).then_inc(s.norm, 1)

        def pre_act(act, k, at):
            there, g, p = at.group(-1)
            if not there:
                return
            s = pre[k]
            act.wait_ge(s.norm, g * 4 + 4)
            for c in range(G):
                last = nc.scalar.activation(h[:, p, c, :], x_all[:, bass.ds(g * G + c, 1), :].rearrange("p a d -> p (a d)"),
                                            ACT.Relu, bias=shift[:, p, c:c + 1], scale=rstd[:, p, c:c + 1])
            last.then_inc(s.h, 1)

        def x_group(g):
            return x_all[:, bass.ds(g * G, G), :]

        def bias_pool(pool, k, at, row):
            there, g, p = at.group(0)
            if not there:
                return
            pool.wait_ge(pre[k].h, g + 1)
            nc.gpsimd.tensor_tensor(x_group(g), x_group(g), row[:, :, :].broadcast_to([N, G, D]), ALU.add).then_inc(pre[k].bias, 1)

        hT0 = sem("hT0")
        hT0_full = sem("hT0_full")
        q_full = sem("q_full")
        k_full = sem("k_full")
        v_full = sem("v_full")
        q_ready = sem("q_ready")
        k_ready = sem("k_ready")
        v_ready = sem("v_ready")
        s0_full = sem("s0_full")
        top0_ready = sem("top0_ready")
        s0_sub = sem("s0_sub")
        p0_ready = sem("p0_ready")
        pT0_full = sem("pT0_full")
        pT0_act = sem("pT0_act")
        pT0_dve = sem("pT0_dve")
        av_full = sem("av_full")
        rsum0_step = sem("rsum0_step")
        att0_ready = sem("att0_ready")
        aT_full = sem("aT_full")
        aT_ready = sem("aT_ready")
        o_full = sem("o_full")
        hd_ready = sem("hd_ready")
        hdT_full = sem("hdT_full")
        hdT_ready = sem("hdT_ready")
        ahT_full = sem("ahT_full")
        ahT_ready = sem("ahT_ready")
        o1_full = sem("o1_full")
        hT2_full = sem("hT2_full")
        hT2 = sem("hT2")
        f_full = sem("f_full")
        lr_step = sem("lr_step")
        s2_full = sem("s2_full")
        scores2 = sem("scores2")
        soft2 = sem("soft2")
        soft2n = sem("soft2n")
        exp2 = sem("exp2")
        pT2_full = sem("pT2_full")
        pT2_ready = [sem("pT2_ready0"), sem("pT2_ready1")]
        agg_full = sem("agg_full")
        agg_act = sem("agg_act")
        agg_dve = sem("agg_dve")
        hd2_full = sem("hd2_full")
        hd2_exp = sem("hd2_exp")
        hd2_elu = sem("hd2_elu")
        wo2_full = sem("wo2_full")
        wh2_act = sem("wh2_act")
        wh2_dve = sem("wh2_dve")
        diag2 = sem("diag2")
        s3_full = sem("s3_full")
        scores3 = sem("scores3")
        top3 = sem("top3")
        exp3 = sem("exp3")
        rsum3_ready = sem("rsum3_ready")
        p3_ready = sem("p3_ready")
        pT3_full = sem("pT3_full")
        pT3_ready = sem("pT3_ready")
        at3_full = sem("at3_full")
        at3_exp = sem("at3_exp")
        at3_elu = sem("at3_elu")
        u_full = sem("u_full")
        u_ready = sem("u_ready")
        y_full = sem("y_full")
        y_step = sem("y_step")
        y_norm = sem("y_norm")
        yn_ready = sem("yn_ready")
        yg_ready = sem("yg_ready")
        hT3_full = sem("hT3_full")
        hT3 = sem("hT3")
        w3_full = sem("w3_full")
        h3_ready = sem("h3_ready")
        diag3 = sem("diag3")
        s4_full = sem("s4_full")
        scores4 = sem("scores4")
        soft4 = sem("soft4")
        exp4 = sem("exp4")
        pT4_full = sem("pT4_full")
        pT4_ready = sem("pT4_ready")
        at4_full = sem("at4_full")
        rsum4 = sem("rsum4")

        block = ctx.enter_context(nc.Block())

        FIRST_LOADS, LATER_LOADS = [], []

        def load(dst, src):
            FIRST_LOADS.append((dst, src))

        load(consts[:, :], shape_consts)
        load(adj_i[:, :], adj)
        for i, w in enumerate((L0_gnn_Wq, L0_gnn_Wk, L0_gnn_Wv, L0_gnn_Wo)):
            load(raw[:, i], w.rearrange("(c p) d -> p c d", p=N))
        for dst, src in ((bq_c, L0_gnn_bq), (bk_c, L0_gnn_bk), (bv_c, L0_gnn_bv), (b1_c, L2_gnn_b1)):
            load(dst[:, :], src)
        load(bo_row[:, 0, :], L0_gnn_bo.partition_broadcast(N))

        def load(dst, src):
            LATER_LOADS.append((dst, src))

        load(raw1, L1_gnn_W.rearrange("(c p) e -> p c e", p=N))
        for dst, src in ((degb_row, L1_gnn_b), (b2_row, L2_gnn_b2),
                         (gamma_row, L2_gnn_ln_gamma), (beta_row, L2_gnn_ln_beta)):
            load(dst[:, 0, :], src.partition_broadcast(N))
        for c in range(KC):
            load(wh[:, c], L2_gnn_W_heads.rearrange("h (c p) o -> p c h o", p=N)[:, c])
        load(a_heads_rows, L2_gnn_a_heads.rearrange("h s -> (h s)").partition_broadcast(N))
        load(wout[:, :, 0:D], L2_gnn_W_out.rearrange("(k p) o -> p k o", p=N))
        load(a_out_rows, L2_gnn_a_out.rearrange("(s d) -> s d", s=2).partition_broadcast(N))
        load(ffn1[:, :, :], L2_gnn_w1.rearrange("(c p) o -> p c o", p=N))
        load(ffn2[:, :, :], L2_gnn_w2.rearrange("(c p) o -> p c o", p=N))
        load(w3[:, :, 0:F3], L3_gnn_W.rearrange("(c p) o -> p c o", p=N))
        load(a3_rows, L3_gnn_a.rearrange("s o e -> s (o e)").partition_broadcast(N))
        LOADED, LATER_LOADED = 16 * len(FIRST_LOADS), 16 * len(LATER_LOADS)

        MASKS_DONE, BV_DONE = 4, 6
        BO_DONE = BV_DONE + 1
        LATE_DONE = 4 + 4 * H2 + 4 + 4

        @block.sync
        def _(sp):
            for dst, src in FIRST_LOADS:
                sp.dma_start(dst, src).then_inc(loads_done, 16)
            for g in range(2):
                sp.dma_start(x_group(g), x_d[:, g * G:(g + 1) * G, :]).then_inc(x_loaded[g], 16)
            for dst, src in LATER_LOADS:
                sp.dma_start(dst, src).then_inc(later_loads_done, 16)
            with sp.Fori(1, NG // 2) as i:
                for p in range(2):
                    sp.wait_ge(x_loaded[p], i * 16)
                    sp.dma_start(x_group(i * 2 + p), x_d[:, bass.ds((i * 2 + p) * G, G), :]).then_inc(x_loaded[p], 16)
            with sp.Fori(0, NG) as g:
                sp.wait_ge(pre[PHASES - 1].x, g + 1)
                sp.dma_start(out_d[:, bass.ds(g * G, G), :], x_group(g)).then_inc(out_stored, 16)
            sp.wait_ge(out_stored, NG * 16)

        @block.gpsimd
        def _(pool):
            nc.gpsimd.memset(pow_half[:, :], -0.5)
            nc.gpsimd.memset(eps_tile[:, :], LN_EPS)
            nc.gpsimd.memset(minus_one[:, :], -1.0)
            nc.gpsimd.memset(ones[:, :], 1.0)
            nc.gpsimd.memset(v1[:, :, :, :, :], 1.0)
            nc.gpsimd.memset(wh_f[:, :, :], 0.0).then_inc(pool_setup, 1)
            pool.wait_ge(pool_setup, 1)

            pool.wait_ge(dve_setup, BO_DONE)

            def step0(at):
                bias_pool(pool, 0, at, bo_row)
                pre_pool(pool, 0, at)

            run_steps(pool, NG, step0)
            if PHASES > 1:
                pool.wait_ge(pre[0].x, NG)
                pool.wait_ge(late_setup, LATE_DONE)

                def step1(at):
                    bias_pool(pool, 1, at, degb_row)
                    pre_pool(pool, 1, at)

                run_steps(pool, NG, step1)
            if PHASES > 2:
                pool.wait_ge(pre[1].x, NG)

                def step2(at):
                    there, g, p = at.group(3)
                    if there:
                        pool.wait_ge(y_step, g * 3 + 3)
                        nc.gpsimd.tensor_tensor(var_y[:, :], mv_y[:, p, :, 1], eps_tile[:, :], ALU.add).then_inc(y_norm, 1)
                        pool.wait_ge(y_norm, g * 2 + 1)
                        nc.gpsimd.tensor_tensor(rstd_y[:, p, :], var_y[:, :], pow_half[:, :], ALU.pow).then_inc(y_norm, 1)
                    bias_pool(pool, 2, at, beta_row)
                    pre_pool(pool, 2, at)
                    if there:
                        pool.wait_ge(yn_ready, g + 1)
                        nc.gpsimd.tensor_tensor(y[:, p], y[:, p], gamma_row[:, :, :].broadcast_to([N, G, D]),
                                                ALU.mult).then_inc(yg_ready, 1)

                run_steps(pool, NG, step2)
            if PHASES > 3:
                pool.wait_ge(pre[2].x, NG)
                run_steps(pool, NG, lambda at: pre_pool(pool, 3, at), 4)


        @block.vector
        def _(dve):
            count = [0]

            def link(ins):
                count[0] += 1
                ins.then_inc(dve_setup, 1)
                dve.wait_ge(dve_setup, count[0])

            dve.wait_ge(loads_done, LOADED)
            dve.wait_ge(pool_setup, 1)
            link(nc.vector.tensor_copy(adj_f[:, :], adj_i[:, :]))
            nc.vector.tensor_copy(ident_bf[:, :], ident)
            for i in range(4):
                nc.vector.tensor_scalar(hide0[:, i, :], adj_f[:, :], 0.0, HIDE, ALU.is_equal, ALU.mult)
            link(nc.vector.tensor_scalar(edge[:, :], adj_f[:, :], 0.0, 0.0, ALU.not_equal, ALU.add, accum_out=edges[:, :]))
            link(nc.vector.reciprocal(poison[:, :], edges[:, :]))
            link(nc.vector.tensor_scalar(poison[:, :], poison[:, :], 0.0, None, ALU.mult))
            assert count[0] == MASKS_DONE
            for c in range(KC):
                link(nc.vector.tensor_scalar(bv_wide[:, c, :], ones[:, :], bv_c[:, c:c + 1], None, ALU.mult))
            assert count[0] == BV_DONE
            for i, dst in ((1, wkT), (3, woT)):
                dve.wait_ge(weights_T, i + 1)
                nc.vector.tensor_copy(dst[:, :, :], bank[i][:, :].rearrange("p (c o) -> p c o", c=2)).then_inc(weights_dve, 1)
            dve.wait_ge(weights_T, 5)
            link(nc.vector.tensor_tensor(bo_row[:, 0, :], bank[7][:, 0:D], bo_row[:, 0, :], ALU.add))
            assert count[0] == BO_DONE

            prod4 = prod[:, 0:KC * D].rearrange("p (c o) -> p c o", c=KC)
            prod8 = prod[:, :].rearrange("p (k o) -> p k o", k=H2 * KC)
            prod3 = prod[:, 0:KC * F3].rearrange("p (c o) -> p c o", c=KC)
            av = a_heads_rows.rearrange("p (h s o) -> p h s o", h=H2, s=2)
            late_count = [0]

            def late(ins):
                late_count[0] += 1
                ins.then_inc(late_setup, 1)
                dve.wait_ge(late_setup, late_count[0])

            def late_part(i):
                if i == 0:
                    dve.wait_ge(later_loads_done, LATER_LOADED)
                    for k in range(4):
                        nc.vector.tensor_scalar(hide2[:, k, :], adj_f[:, :], 0.0, HIDE, ALU.is_le, ALU.mult)
                    late(nc.vector.reduce_sum(deg[:, :], adj_f[:, :], AX.X))
                    late(nc.vector.tensor_scalar(degb_row[:, 0, :], degb_row[:, 0, :], deg[:, :], None, ALU.mult))
                    late(nc.vector.tensor_scalar(neg3[:, :], adj_f[:, :], -1.0, 1.0, ALU.mult, ALU.add))
                    late(nc.vector.tensor_scalar(neg3[:, :], neg3[:, :], NEG, None, ALU.mult))
                if i in (1, 2):
                    s = i - 1
                    for hh in range(H2):
                        late(nc.vector.tensor_tensor(prod4, wh[:, :, hh, :], av[:, hh, s:s + 1, :].broadcast_to([N, KC, D]), ALU.mult))
                        late(nc.vector.reduce_sum(wh_f[:, :, s * H2 + hh], prod4, AX.X))
                if i in (0, 3):
                    s = i // 3
                    late(nc.vector.tensor_tensor(prod8, wout[:, :, 0:D], a_out_rows[:, s:s + 1, :].broadcast_to([N, H2 * KC, D]), ALU.mult))
                    late(nc.vector.reduce_sum(wout[:, :, D + s], prod8, AX.X))
                if i == 3:
                    for s in range(2):
                        late(nc.vector.tensor_tensor(prod3, w3[:, :, 0:F3], a3_rows[:, s:s + 1, :].broadcast_to([N, KC, F3]), ALU.mult))
                        late(nc.vector.reduce_sum(w3[:, :, F3 + s], prod3, AX.X))

            def step0(at):
                f, g, p = at.group(0)
                b, gb, pb = at.group(1)
                if f:
                    dve.wait_ge(q_full, g + 1)
                    if positive(g):
                        dve.wait_ge(s0_full, g * 4)
                    for c in range(KC):
                        last = nc.vector.tensor_scalar(qT[:, c], bank[1][:, c * 256:(c + 1) * 256].rearrange("p (c n) -> p c n", c=G),
                                                       bq_c[:, c:c + 1], None, ALU.add)
                    last.then_inc(q_ready, 1)
                if b:
                    for k, r in enumerate((1, 3)):
                        dve.wait_ge(pT0_full, gb * 4 + r + 1)
                        if positive(gb) and k == 0:
                            dve.wait_ge(av_full, gb * 2)
                        nc.vector.tensor_copy(probsT[:, r], bank[3][:, :].rearrange("p (k n) -> p k n", k=4)).then_inc(pT0_dve, 1)
                pre_dve(dve, 0, at)
                if not b:
                    stats_written(dve, 0, at)
                    moments_dve(0, at)
                if b:
                    dve.wait_ge(av_full, gb * 2 + 2)
                    stats_written(dve, 0, at)
                    for c in range(G):
                        o = bank[2 + c][:, 0:H0 * (DH + 1)].rearrange("p (h e) -> p h e", h=H0)
                        last = nc.vector.reciprocal(rsum0[:, c, :], o[:, :, DH])
                    last.then_inc(rsum0_step, 1)
                    moments_dve(0, at)
                    dve.wait_ge(rsum0_step, gb * 2 + 1)
                    nc.vector.tensor_scalar(rsum0[:, :, :], rsum0[:, :, :], poison[:, :], None, ALU.add).then_inc(rsum0_step, 1)
                    dve.wait_ge(rsum0_step, gb * 2 + 2)
                    if positive(gb):
                        dve.wait_ge(aT_full, gb)
                    for c in range(G):
                        o = bank[2 + c][:, 0:H0 * (DH + 1)].rearrange("p (h e) -> p h e", h=H0)
                        last = nc.vector.tensor_tensor(att0[:, c], o[:, :, 0:DH],
                                                       rsum0[:, c, :].unsqueeze(2).broadcast_to([N, H0, DH]), ALU.mult)
                    last.then_inc(att0_ready, 1)
                if f:
                    for u in range(2):
                        for r in (2 * u, 2 * u + 1):
                            dve.wait_ge(s0_full, g * 4 + r + 1)
                            last = nc.vector.reduce_max(top0[:, r, :], bank[4 + r][:, :].rearrange("p (k n) -> p k n", k=4), AX.X)
                        last.then_inc(top0_ready, 1)
                        dve.wait_ge(top0_ready, g * 2 + u + 1)
                        if positive(g) and u == 0:
                            dve.wait_ge(pT0_full, g * 4)
                        for r in (2 * u, 2 * u + 1):
                            last = nc.vector.tensor_tensor(probs[:, r], bank[4 + r][:, :].rearrange("p (k n) -> p k n", k=4),
                                                           top0[:, r, :].unsqueeze(2).broadcast_to([N, 4, N]), ALU.subtract)
                        last.then_inc(s0_sub, 1)
                if b:
                    dve.wait_ge(o_full, gb + 1)
                    dve.wait_ge(pre[0].bias, gb + 1)
                    nc.vector.tensor_tensor(x_group(gb), bank[3][:, :].rearrange("p (c d) -> p c d", c=G), x_group(gb),
                                            ALU.add).then_inc(pre[0].x, 1)
                if isinstance(at.t, int) and 0 <= at.t < 4:
                    late_part(at.t)

            run_steps(dve, NG, step0)
            assert late_count[0] == LATE_DONE

            def step1(at):
                pre_dve(dve, 1, at)
                f, g, p = at.group(0)
                b, gb, pb = at.group(1)
                stats_written(dve, 1, at)
                if f:
                    dve.wait_ge(ahT_full, g + 1)
                    if positive(g - 1):
                        dve.wait_ge(o1_full, g - 1)
                    nc.vector.tensor_copy(ahT[:, p], bank[2 + p][:, :].rearrange("p (k c n) -> p k c n", k=KC, c=G)).then_inc(ahT_ready, 1)
                moments_dve(1, at)
                n, gn, pn = at.group(-1)
                if n:
                    dve.wait_ge(pre[1].h, gn + 1)
                    if positive(gn - 1):
                        dve.wait_ge(hdT_full, gn - 1)
                    nc.vector.tensor_scalar(hd[:, pn], h[:, pn], deg[:, :], None, ALU.mult).then_inc(hd_ready, 1)
                if b:
                    dve.wait_ge(o1_full, gb + 1)
                    dve.wait_ge(pre[1].bias, gb + 1)
                    nc.vector.tensor_tensor(x_group(gb), bank[4 + pb][:, :].rearrange("p (c d) -> p c d", c=G), x_group(gb),
                                            ALU.add).then_inc(pre[1].x, 1)

            if PHASES > 1:
                dve.wait_ge(pre[0].x, NG)
                run_steps(dve, NG, step1)

            def step2(at):
                f, g, p = at.group(0)
                m, gm, pm = at.group(1)
                l, gl, pl = at.group(2)
                e, ge, pe_ = at.group(3)
                if e:
                    dve.wait_ge(y_step, ge * 3 + 2)
                if f:
                    dve.wait_ge(hT2_full, g + 1)
                    if positive(g):
                        dve.wait_ge(f_full, g)
                    nc.vector.tensor_copy(hT[:, :, :, :], bank[0][:, :].rearrange("p (k c n) -> p k c n", k=KC, c=G)).then_inc(hT2, 1)
                if m:
                    dve.wait_ge(pT2_full, gm * 2 + 2)
                    if positive(gm):
                        dve.wait_ge(agg_full, gm * 4)
                    nc.vector.tensor_copy(probsT[:, 1], bank[4][:, :].rearrange("p (h n) -> p h n", h=H2)).then_inc(pT2_ready[1], 1)
                if e:
                    for c in range(G):
                        last = nc.vector.bn_aggr(mv_y[:, pe_, c, :], st_y[:, c, :])
                    last.then_inc(y_step, 1)
                if m:
                    for k, i in enumerate((1, 3)):
                        dve.wait_ge(agg_full, gm * 4 + i + 1)
                        if positive(gm) and k == 0:
                            dve.wait_ge(hd2_full, gm * 4)
                        c, dc = i // 2, i % 2
                        nc.vector.tensor_copy(aggT[:, dc, :, c, :], bank[3 + (2 + i) % 4][:, :].rearrange("p (h n) -> p h n", h=H2)).then_inc(agg_dve, 1)
                if f:
                    dve.wait_ge(f_full, g + 1)
                    if positive(g):
                        dve.wait_ge(s2_full, g * 2)
                    nc.vector.tensor_scalar(left[:, :], bank[0][0:64, 0:N], left_mul[0:64], left_add[0:64], ALU.mult, ALU.add)
                    nc.vector.tensor_scalar(right_rows[:, :], bank[0][0:64, 0:N], right_mul[0:64], right_add[0:64],
                                            ALU.mult, ALU.add).then_inc(lr_step, 1)
                    dve.wait_ge(lr_step, g * 2 + 1)
                    nc.vector.tensor_tensor(right[:, :, :], right_rows[:, :].unsqueeze(1).broadcast_to([64, H2, N]),
                                            head_rows[0:64], ALU.mult).then_inc(lr_step, 1)
                if l:
                    dve.wait_ge(scores3, gl + 1)
                    nc.vector.scalar_tensor_tensor(t3[:, 0], t3[:, 0], LEAK2, t3[:, 0], ALU.mult, ALU.max).then_inc(top3, 1)
                    dve.wait_ge(top3, gl * 2 + 1)
                    nc.vector.tensor_reduce(negtop[:, :], t3[:, 0], AX.X, ALU.max, negate=True).then_inc(top3, 1)

                def elu_head(i):
                    dve.wait_ge(hd2_exp, gm * 4 + i + 1)
                    nc.vector.tensor_scalar(em[:, i % 2], em[:, i % 2], 1.0, -1.0, ALU.min, ALU.add).then_inc(hd2_elu, 1)
                    dve.wait_ge(hd2_elu, gm * 8 + 2 * i + 1)
                    if positive(gm) and i == 0:
                        dve.wait_ge(wo2_full, gm * 2)
                    nc.vector.tensor_tensor(headsT[:, i].rearrange("p k c n -> p k (c n)"),
                                            bank[3 + (6 + i) % 4][:, :].rearrange("p (k n) -> p k n", k=KC), em[:, i % 2],
                                            ALU.max).then_inc(hd2_elu, 1)

                def soft(c):
                    n0 = g * 6 + c * 3
                    dve.wait_ge(scores2, g * 2 + c + 1)
                    nc.vector.scalar_tensor_tensor(probs[:, c], probs[:, c], LEAK2, probs[:, c], ALU.mult, ALU.max).then_inc(soft2, 1)
                    dve.wait_ge(soft2, n0 + 1)
                    nc.vector.reduce_max(top2[:, c, :], probs[:, c], AX.X).then_inc(soft2, 1)
                    dve.wait_ge(soft2, n0 + 2)
                    nc.vector.tensor_tensor(probs[:, c], probs[:, c], top2[:, c, :].unsqueeze(2).broadcast_to([N, H2, N]),
                                            ALU.subtract).then_inc(soft2, 1)

                def normalise(c):
                    dve.wait_ge(exp2, g * 2 + c + 1)
                    nc.vector.reduce_sum(sum2[:, c, :], probs[:, c], AX.X).then_inc(soft2n, 1)
                    dve.wait_ge(soft2n, g * 6 + c * 3 + 1)
                    nc.vector.reciprocal(rsum2[:, c, :], sum2[:, c, :]).then_inc(soft2n, 1)
                    dve.wait_ge(soft2n, g * 6 + c * 3 + 2)
                    nc.vector.tensor_tensor(probs[:, c], probs[:, c], rsum2[:, c, :].unsqueeze(2).broadcast_to([N, H2, N]),
                                            ALU.mult).then_inc(soft2n, 1)

                if m:
                    elu_head(0)
                if l:
                    dve.wait_ge(exp3, gl + 1)
                    nc.vector.reciprocal(rsum3[:, :], sum3[:, 0, :]).then_inc(rsum3_ready, 1)
                    dve.wait_ge(rsum3_ready, gl + 1)
                    for c in range(G):
                        last = nc.vector.tensor_scalar(t3[:, 0, c, :], t3[:, 0, c, :], rsum3[:, c:c + 1], None, ALU.mult)
                    last.then_inc(p3_ready, 1)
                pre_dve(dve, 2, at)
                stats_written(dve, 2, at)
                if m:
                    elu_head(1)
                moments_dve(2, at)
                if e:
                    dve.wait_ge(y_norm, ge * 2 + 2)
                    for c in range(G):
                        last = nc.vector.tensor_scalar(y[:, pe_, c, :], y[:, pe_, c, :], mv_y[:, pe_, c, 0:1], rstd_y[:, pe_, c:c + 1],
                                                       ALU.subtract, ALU.mult)
                    last.then_inc(yn_ready, 1)
                if f:
                    soft(0)
                if m:
                    elu_head(2)
                if m:
                    elu_head(3)
                if f:
                    soft(1)
                if l:
                    dve.wait_ge(at3_exp, gl + 1)
                    nc.vector.tensor_scalar(em3[:, :, :, :], em3[:, :, :, :], 1.0, -1.0, ALU.min, ALU.add).then_inc(at3_elu, 1)
                    dve.wait_ge(at3_elu, gl * 2 + 1)
                    if positive(gl):
                        dve.wait_ge(y_full, gl)
                    nc.vector.tensor_tensor(outT[:, :, :, :], bank[7][:, :].rearrange("p (k c n) -> p k c n", k=KC, c=G),
                                            em3[:, :, :, :], ALU.max).then_inc(at3_elu, 1)
                if f:
                    normalise(0)
                    normalise(1)
                if e:
                    dve.wait_ge(yg_ready, ge + 1)
                    dve.wait_ge(pre[2].bias, ge + 1)
                    nc.vector.tensor_tensor(x_group(ge), x_group(ge), y[:, pe_], ALU.add).then_inc(pre[2].x, 1)
                if m:
                    dve.wait_ge(wo2_full, gm * 2 + 2)
                    if positive(gm):
                        dve.wait_ge(at3_full, gm)
                    nc.vector.tensor_copy(wh2[:, 1, :], bank[3 + 11 % 4][:, 0:D + 2]).then_inc(wh2_dve, 1)
                if m:
                    dve.wait_ge(wh2_dve, gm + 1)
                    dve.wait_ge(wh2_act, gm + 1)
                    for c in range(G):
                        last = nc.vector.tensor_scalar(diag[:, 0, c, :], ident, wh2[:, c, D + 1:D + 2], None, ALU.mult)
                    last.then_inc(diag2, 1)
                if l:
                    dve.wait_ge(y_full, gl + 1)
                    nc.vector.tensor_tensor(y[:, pl], bank[7][:, :].rearrange("p (c d) -> p c d", c=G),
                                            b2_row[:, :, :].broadcast_to([N, G, D]), ALU.add).then_inc(y_step, 1)
                    dve.wait_ge(y_step, gl * 3 + 1)
                    for c in range(G):
                        last = nc.vector.bn_stats(st_y[:, c, :], y[:, pl, c, :])
                    last.then_inc(y_step, 1)

            if PHASES > 2:
                dve.wait_ge(pre[1].x, NG)
                run_steps(dve, NG, step2)

            def step3(at):
                n, gn, _ = at.group(-1)
                f, g, p = at.group(0)
                m, gm, pm = at.group(1)
                e, ge, pe_ = at.group(3)
                pre_dve(dve, 3, at)
                if e:
                    dve.wait_ge(at4_full, ge + 1)
                    if positive(ge):
                        dve.wait_ge(pre[3].x, ge)
                    nc.vector.reciprocal(rsum3[:, :], sum3[:, pe_, :]).then_inc(rsum4, 1)
                if m:
                    xs = x_all[:, bass.ds(gm * G, G), F3:D]
                    nc.vector.tensor_tensor(xs, xs, h3[:, at.quarter(1), :, 0:F3], ALU.add)
                stats_written(dve, 3, at)
                if e:
                    dve.wait_ge(rsum4, ge + 1)
                    for c in range(G):
                        xs = x_all[:, bass.ds(ge * G + c, 1), 0:F3].rearrange("p a d -> p (a d)")
                        last = nc.vector.scalar_tensor_tensor(xs, bank[4][:, c * F3:(c + 1) * F3], rsum3[:, c:c + 1], xs, ALU.mult, ALU.add)
                    last.then_inc(pre[3].x, 1)
                moments_dve(3, at)
                if m:
                    dve.wait_ge(scores4, gm + 1)
                    nc.vector.scalar_tensor_tensor(t3[:, pm], t3[:, pm], LEAK3, t3[:, pm], ALU.mult, ALU.max).then_inc(soft4, 1)
                    dve.wait_ge(soft4, gm * 3 + 1)
                    nc.vector.tensor_tensor(t3[:, pm], t3[:, pm], neg3[:, :].unsqueeze(1).broadcast_to([N, G, N]), ALU.add).then_inc(soft4, 1)
                if f:
                    dve.wait_ge(h3_ready, g + 1)
                    if positive(g - 1):
                        dve.wait_ge(s4_full, g - 1)
                    for c in range(G):
                        last = nc.vector.tensor_scalar(diag[:, p, c, :], ident, h3[:, at.quarter(0), c, F3 + 1:F3 + 2], None, ALU.mult)
                    last.then_inc(diag3, 1)
                if m:
                    dve.wait_ge(soft4, gm * 3 + 2)
                    nc.vector.tensor_reduce(negtop[:, :], t3[:, pm], AX.X, ALU.max, negate=True).then_inc(soft4, 1)
                if n:
                    dve.wait_ge(hT3_full, gn + 1)
                    if positive(gn):
                        dve.wait_ge(w3_full, gn)
                    nc.vector.tensor_copy(hT[:, :, :, :], bank[0][:, :].rearrange("p (k c n) -> p k c n", k=KC, c=G)).then_inc(hT3, 1)

            if PHASES > 3:
                dve.wait_ge(pre[2].x, NG)
                run_steps(dve, NG, step3, 4)

        @block.scalar
        def _(act):
            def step0(at):
                f, g, p = at.group(0)
                b, gb, pb = at.group(1)

                def probs_T(r):
                    act.wait_ge(pT0_full, gb * 4 + r + 1)
                    if positive(gb) and r == 0:
                        act.wait_ge(av_full, gb * 2)
                    nc.scalar.copy(probsT[:, r], bank[2][:, :].rearrange("p (k n) -> p k n", k=4)).then_inc(pT0_act, 1)

                if b:
                    probs_T(0)
                if f:
                    act.wait_ge(k_full, g + 1)
                    if positive(g):
                        act.wait_ge(s0_full, g * 4)
                    for c in range(KC):
                        last = nc.scalar.activation(kT[:, c], bank[0][:, c * 256:(c + 1) * 256].rearrange("p (c n) -> p c n", c=G),
                                                    ACT.Identity, bias=bk_c[:, c:c + 1])
                    last.then_inc(k_ready, 1)
                if b:
                    probs_T(2)
                n, gn, _ = at.group(-1)
                if n and positive(gn - 1):
                    act.wait_ge(hT0_full, gn - 1)
                pre_act(act, 0, at)
                if f:
                    act.wait_ge(v_full, g + 1)
                    if positive(g - 1):
                        act.wait_ge(av_full, (g - 1) * 2)
                    nc.scalar.copy(v1[:, p, :, :, 0:DH].rearrange("p c h e -> p (c h) e"),
                                   bank[1][:, :].rearrange("p (k e) -> p k e", e=DH)).then_inc(v_ready, 1)
                n, gn, _ = at.group(-1)
                if n:
                    act.wait_ge(hT0_full, gn + 1)
                    if positive(gn):
                        act.wait_ge(v_full, gn)
                    nc.scalar.copy(hT[:, :, :, :], bank[0][:, :].rearrange("p (k c n) -> p k c n", k=KC, c=G)).then_inc(hT0, 1)
                if b:
                    act.wait_ge(aT_full, gb + 1)
                    if positive(gb):
                        act.wait_ge(o_full, gb)
                    nc.scalar.copy(att0T[:, :, :, :], bank[2][:, :].rearrange("p (k c n) -> p k c n", k=KC, c=G)).then_inc(aT_ready, 1)
                if f:
                    for u in range(2):
                        act.wait_ge(s0_sub, g * 2 + u + 1)
                        nc.scalar.activation(probs[:, 2 * u:2 * u + 2], probs[:, 2 * u:2 * u + 2], ACT.Exp,
                                             scale=float(DH) ** -0.5).then_inc(p0_ready, 1)

            act.wait_ge(pool_setup, 1)
            act.wait_ge(loads_done, LOADED)
            for i, dst in ((0, wqT), (2, wvT)):
                act.wait_ge(weights_T, i + 1)
                nc.scalar.copy(dst[:, :, :], bank[i][:, :].rearrange("p (c o) -> p c o", c=2)).then_inc(weights_act, 1)
            run_steps(act, NG, step0)

            def step1(at):
                f, g, p = at.group(0)
                if f:
                    act.wait_ge(hdT_full, g + 1)
                    if positive(g - 1):
                        act.wait_ge(o1_full, g - 1)
                    nc.scalar.copy(hdT[:, p], bank[p][:, :].rearrange("p (k c n) -> p k c n", k=KC, c=G)).then_inc(hdT_ready, 1)
                n, gn, _ = at.group(-1)
                if n and positive(gn - 1):
                    act.wait_ge(ahT_full, gn - 1)
                pre_act(act, 1, at)

            if PHASES > 1:
                act.wait_ge(pre[0].x, NG)
                act.wait_ge(weights_T, 6)
                nc.scalar.copy(adjT[:, :], bank[6][:, 0:N]).then_inc(weights_act, 1)
                for i in range(2):
                    act.wait_ge(weights_T, 7 + i)
                    nc.scalar.copy(w1T[:, i * 2:i * 2 + 2, :], bank[4 + i][:, :].rearrange("p (c o) -> p c o", c=2)).then_inc(weights_act, 1)
                run_steps(act, NG, step1)

            def step2(at):
                f, g, p = at.group(0)
                m, gm, pm = at.group(1)
                l, gl, pl = at.group(2)
                if m:
                    act.wait_ge(pT2_full, gm * 2 + 1)
                    if positive(gm):
                        act.wait_ge(agg_full, gm * 4)
                    nc.scalar.copy(probsT[:, 0], bank[3][:, :].rearrange("p (h n) -> p h n", h=H2)).then_inc(pT2_ready[0], 1)
                    for k, i in enumerate((0, 2)):
                        act.wait_ge(agg_full, gm * 4 + i + 1)
                        if positive(gm) and k == 0:
                            act.wait_ge(hd2_full, gm * 4)
                        c, dc = i // 2, i % 2
                        nc.scalar.copy(aggT[:, dc, :, c, :], bank[3 + (2 + i) % 4][:, :].rearrange("p (h n) -> p h n", h=H2)).then_inc(agg_act, 1)
                if l:
                    act.wait_ge(s3_full, gl + 1)
                    act.wait_ge(wh2_dve, gl + 1)
                    act.wait_ge(wh2_act, gl + 1)
                    if positive(gl):
                        act.wait_ge(pT3_full, gl)
                    for c in range(G):
                        last = nc.scalar.activation(t3[:, 0, c, :], bank[7][:, c * N:(c + 1) * N], ACT.Identity,
                                                    bias=wh2[:, c, D:D + 1])
                    last.then_inc(scores3, 1)

                def exp_head(i):
                    act.wait_ge(hd2_full, gm * 4 + i + 1)
                    if i >= 2:
                        act.wait_ge(hd2_elu, gm * 8 + 2 * i - 2)
                    elif positive(gm):
                        act.wait_ge(hd2_elu, gm * 8 + 2 * i - 2)
                    nc.scalar.activation(em[:, i % 2], bank[3 + (6 + i) % 4][:, :].rearrange("p (k n) -> p k n", k=KC),
                                         ACT.Exp).then_inc(hd2_exp, 1)

                def scores_out(c):
                    act.wait_ge(s2_full, g * 2 + c + 1)
                    if positive(g) and c == 0:
                        act.wait_ge(pT2_full, g * 2)
                    nc.scalar.activation(probs[:, c], bank[1 + c][:, :].rearrange("p (h n) -> p h n", h=H2),
                                         ACT.Identity).then_inc(scores2, 1)

                def exp_scores(c):
                    act.wait_ge(soft2, g * 6 + c * 3 + 3)
                    nc.scalar.activation(probs[:, c], probs[:, c], ACT.Exp).then_inc(exp2, 1)

                if m:
                    exp_head(0)
                if l:
                    act.wait_ge(top3, gl * 2 + 2)
                    for c in range(G):
                        last = nc.scalar.activation(t3[:, 0, c, :], t3[:, 0, c, :], ACT.Exp, bias=negtop[:, c:c + 1],
                                                    accum_out=sum3[:, 0, c:c + 1])
                    last.then_inc(exp3, 1)
                if m:
                    exp_head(1)
                n, gn, _ = at.group(-1)
                if n and positive(gn - 1):
                    act.wait_ge(agg_full, (gn - 1) * 4)
                pre_act(act, 2, at)
                if f:
                    scores_out(0)
                    scores_out(1)
                if l:
                    act.wait_ge(pT3_full, gl + 1)
                    if positive(gl):
                        act.wait_ge(at3_full, gl)
                    nc.scalar.copy(p3T[:, :, :], bank[7][:, 0:G * N].rearrange("p (c n) -> p c n", c=G)).then_inc(pT3_ready, 1)
                if m:
                    exp_head(2)
                    exp_head(3)
                if f:
                    exp_scores(0)
                if l:
                    act.wait_ge(at3_full, gl + 1)
                    if positive(gl):
                        act.wait_ge(at3_elu, gl * 2)
                    nc.scalar.activation(em3[:, :, :, :], bank[7][:, :].rearrange("p (k c n) -> p k c n", k=KC, c=G),
                                         ACT.Exp).then_inc(at3_exp, 1)
                if f:
                    exp_scores(1)
                if m:
                    act.wait_ge(wo2_full, gm * 2 + 1)
                    if positive(gm):
                        act.wait_ge(at3_full, gm)
                    nc.scalar.copy(wh2[:, 0, :], bank[3 + 10 % 4][:, 0:D + 2]).then_inc(wh2_act, 1)
                if l:
                    act.wait_ge(u_full, gl + 1)
                    if positive(gl):
                        act.wait_ge(y_full, gl)
                    for c in range(KC):
                        last = nc.scalar.activation(uT[:, c], bank[7][:, c * 256:(c + 1) * 256].rearrange("p (c n) -> p c n", c=G),
                                                    ACT.Relu, bias=b1_c[:, c:c + 1])
                    last.then_inc(u_ready, 1)

            if PHASES > 2:
                act.wait_ge(pre[1].x, NG)
                run_steps(act, NG, step2)

            def step3(at):
                f, g, p = at.group(0)
                m, gm, pm = at.group(1)
                l, gl, pl = at.group(2)
                if m:
                    act.wait_ge(s4_full, gm + 1)
                    if positive(gm - 1):
                        act.wait_ge(pT4_full, gm - 1)
                    for c in range(G):
                        last = nc.scalar.activation(t3[:, pm, c, :], bank[2][:, c * N:(c + 1) * N], ACT.Identity,
                                                    bias=h3[:, at.quarter(1), c, F3:F3 + 1])
                    last.then_inc(scores4, 1)
                if l:
                    act.wait_ge(pT4_full, gl + 1)
                    if positive(gl):
                        act.wait_ge(at4_full, gl)
                    nc.scalar.copy(p3T[:, :, :], bank[3][:, 0:G * N].rearrange("p (c n) -> p c n", c=G)).then_inc(pT4_ready, 1)
                if f:
                    act.wait_ge(w3_full, g + 1)
                    if positive(g - 3):
                        act.wait_ge(at4_full, g - 3)
                    nc.scalar.copy(h3[:, at.quarter(0)], bank[1][:, 0:G * (F3 + 2)].rearrange("p (c d) -> p c d", c=G)).then_inc(h3_ready, 1)
                n, gn, _ = at.group(-1)
                if n and positive(gn - 1):
                    act.wait_ge(hT3_full, gn - 1)
                pre_act(act, 3, at)
                if m:
                    act.wait_ge(soft4, gm * 3 + 3)
                    if positive(gm - 1):
                        act.wait_ge(rsum4, gm - 1)
                    for c in range(G):
                        last = nc.scalar.activation(t3[:, pm, c, :], t3[:, pm, c, :], ACT.Exp, bias=negtop[:, c:c + 1],
                                                    accum_out=sum3[:, pm, c:c + 1])
                    last.then_inc(exp4, 1)

            if PHASES > 3:
                act.wait_ge(pre[2].x, NG)
                run_steps(act, NG, step3, 4)

        @block.tensor
        def _(pe):
            pe.wait_ge(loads_done, LOADED)
            for i in range(4):
                for k in range(KC):
                    for c in range(KC):
                        last = nc.tensor.transpose(bank[i][:, (k * KC + c) * N:(k * KC + c + 1) * N], raw[:, i, c, k * N:(k + 1) * N], ident)
                last.then_inc(weights_T, 1)
            pe.wait_ge(dve_setup, BV_DONE)
            pe.wait_ge(weights_dve, 2)
            for k in range(KC):
                last = nc.tensor.matmul(bank[7][:, 0:D], bv_wide[:, k, :], woT[:, k, :], start=(k == 0), stop=(k == KC - 1))
            last.then_inc(weights_T, 1)
            pe.wait_ge(weights_act, 2)
            pe.wait_ge(dve_setup, BO_DONE)

            def transpose_group(dst, src):
                for k in range(KC):
                    for c in range(G):
                        last = nc.tensor.transpose(dst[:, (k * G + c) * N:(k * G + c + 1) * N], src[:, c, k * N:(k + 1) * N], ident)
                return last

            def step0(at):
                f, g, p = at.group(0)
                b, gb, pb = at.group(1)

                def project_T(dst, w):
                    for o in range(KC):
                        for k in range(KC):
                            last = nc.tensor.matmul(dst[:, o * G * N:(o + 1) * G * N], w[:, k, o * N:(o + 1) * N],
                                                    hT[:, k].rearrange("p c n -> p (c n)"), start=(k == 0), stop=(k == KC - 1))
                    return last

                def probs_T(r, first):
                    pe.wait_ge(p0_ready, gb * 2 + r // 2 + 1)
                    if first is not None:
                        pe.wait_ge(*first)
                    for k in range(4):
                        last = nc.tensor.transpose(bank[2 + r % 2][:, k * N:(k + 1) * N], probs[:, r, k, :], ident)
                    last.then_inc(pT0_full, 1)

                if f:
                    pe.wait_ge(hT0, g + 1)
                    if positive(g):
                        pe.wait_ge(v_ready, g)
                    project_T(bank[1], wqT).then_inc(q_full, 1)
                if b:
                    probs_T(0, (aT_ready, gb) if positive(gb) else None)
                    probs_T(1, (pre[0].x, gb) if positive(gb) else None)
                if f:
                    project_T(bank[0], wkT).then_inc(k_full, 1)
                if b:
                    probs_T(2, (pT0_act, gb * 2 + 1))
                    probs_T(3, (pT0_dve, gb * 2 + 1))
                if f:
                    pe.wait_ge(q_ready, g + 1)
                    for c in range(G):
                        for k in range(KC):
                            last = nc.tensor.matmul(bank[1][:, c * D:(c + 1) * D], hT[:, k, c, :], wvT[:, k, :],
                                                    start=(k == 0), stop=(k == KC - 1))
                    last.then_inc(v_full, 1)
                if b:
                    pe.wait_ge(pT0_act, gb * 2 + 2)
                    pe.wait_ge(pT0_dve, gb * 2 + 2)
                    for c in range(G):
                        for hh in range(H0):
                            last = nc.tensor.matmul(bank[2 + c][:, hh * (DH + 1):(hh + 1) * (DH + 1)],
                                                    probsT[:, hh % 4, (hh // 4) * G + c, :], v1[:, pb, c, hh, :], start=True, stop=True)
                        last.then_inc(av_full, 1)
                n, gn, pn = at.group(-1)
                if n:
                    pe.wait_ge(pre[0].h, gn + 1)
                    if positive(gn):
                        pe.wait_ge(k_ready, gn)
                    transpose_group(bank[0], h[:, pn]).then_inc(hT0_full, 1)

                def scores(k):
                    for c in range(G):
                        for r in range(4):
                            i = k * G + c
                            rows = slice(r * DH, (r + 1) * DH)
                            last = nc.tensor.matmul(bank[4 + r][:, i * N:(i + 1) * N], qT[rows, k, c, :], kT[rows, k, c, :],
                                                    start=False, stop=(i == KC * G - 1))
                            if i == KC * G - 1:
                                last.then_inc(s0_full, 1)

                if f:
                    pe.wait_ge(k_ready, g + 1)
                    pe.wait_ge(v_ready, g + 1)
                    if positive(g):
                        pe.wait_ge(s0_sub, g * 2)
                    for r in range(4):
                        nc.tensor.matmul(bank[4 + r][:, :], ident_bf[:, :], hide0[:, :, :], start=True, stop=False)
                    scores(0)
                if b:
                    pe.wait_ge(att0_ready, gb + 1)
                    transpose_group(bank[2], att0[:, :].rearrange("p c h e -> p c (h e)")).then_inc(aT_full, 1)
                if f:
                    scores(1)
                if b:
                    pe.wait_ge(aT_ready, gb + 1)
                    for c in range(G):
                        for k in range(KC):
                            last = nc.tensor.matmul(bank[3][:, c * D:(c + 1) * D], att0T[:, k, c, :], woT[:, k, :],
                                                    start=(k == 0), stop=(k == KC - 1))
                    last.then_inc(o_full, 1)

            run_steps(pe, NG, step0)

            def step1(at):
                f, g, p = at.group(0)
                b, gb, pb = at.group(1)
                if f:
                    pe.wait_ge(hd_ready, g + 1)
                    if positive(g - 1):
                        pe.wait_ge(hdT_ready, g - 1)
                    transpose_group(bank[p], hd[:, p]).then_inc(hdT_full, 1)
                    if positive(g - 1):
                        pe.wait_ge(ahT_ready, g - 1)
                    for k in range(KC):
                        for c in range(G):
                            last = nc.tensor.matmul(bank[2 + p][:, (k * G + c) * N:(k * G + c + 1) * N], h[:, p, c, k * N:(k + 1) * N],
                                                    adjT[:, :], start=True, stop=True)
                    last.then_inc(ahT_full, 1)
                if b:
                    pe.wait_ge(hdT_ready, gb + 1)
                    pe.wait_ge(ahT_ready, gb + 1)
                    if positive(gb - 1):
                        pe.wait_ge(pre[1].x, gb - 1)
                    for c in range(G):
                        for k in range(2 * KC):
                            src = hdT[:, pb, k, c, :] if k < KC else ahT[:, pb, k - KC, c, :]
                            last = nc.tensor.matmul(bank[4 + pb][:, c * D:(c + 1) * D], src, w1T[:, k, :],
                                                    start=(k == 0), stop=(k == 2 * KC - 1))
                    last.then_inc(o1_full, 1)

            if PHASES > 1:
                pe.wait_ge(pre[0].x, NG)
                pe.wait_ge(later_loads_done, LATER_LOADED)
                nc.tensor.transpose(bank[6][:, 0:N], adj_f[:, :], ident).then_inc(weights_T, 1)
                for i in range(2):
                    for k in range(KC):
                        for c in range(KC):
                            last = nc.tensor.transpose(bank[4 + i][:, (k * KC + c) * N:(k * KC + c + 1) * N],
                                                       raw1[:, c, (i * KC + k) * N:(i * KC + k + 1) * N], ident)
                    last.then_inc(weights_T, 1)
                pe.wait_ge(weights_act, 5)
                run_steps(pe, NG, step1)

            def step2(at):
                f, g, p = at.group(0)
                m, gm, pm = at.group(1)
                l, gl, pl = at.group(2)
                if f:
                    pe.wait_ge(pre[2].h, g + 1)
                    if positive(g):
                        pe.wait_ge(lr_step, g * 2)
                    transpose_group(bank[0], h[:, p]).then_inc(hT2_full, 1)
                if m:
                    for c in range(G):
                        pe.wait_ge(soft2n, gm * 6 + c * 3 + 3)
                        if c == 0 and positive(gm):
                            pe.wait_ge(hd2_elu, gm * 8)
                        for hh in range(H2):
                            last = nc.tensor.transpose(bank[3 + c][:, hh * N:(hh + 1) * N], probs[:, c, hh, :], ident)
                        last.then_inc(pT2_full, 1)
                    for i in range(4):
                        c, dc = i // 2, i % 2
                        if i == 0:
                            if positive(gm):
                                pe.wait_ge(wh2_act, gm)
                                pe.wait_ge(wh2_dve, gm)
                            pe.wait_ge(pT2_ready[0], gm + 1)
                        if i == 2:
                            pe.wait_ge(pT2_ready[1], gm + 1)
                        last = nc.tensor.matmul(bank[3 + (2 + i) % 4][:, :], h[:, pm, c, dc * N:(dc + 1) * N],
                                                probsT[:, c].rearrange("p h n -> p (h n)"), start=True, stop=True)
                        last.then_inc(agg_full, 1)
                if l:
                    pe.wait_ge(diag2, gl + 1)
                    if positive(gl):
                        pe.wait_ge(y_step, gl * 3 - 2)
                    nc.tensor.matmul(bank[7][:, 0:G * N], ident_bf[:, :], hide2[:, 0:G, :], start=True, stop=False)
                    nc.tensor.matmul(bank[7][:, 0:G * N], ones[:, :], diag[:, 0].rearrange("p c n -> p (c n)"),
                                     start=False, stop=True).then_inc(s3_full, 1)
                if f:
                    pe.wait_ge(hT2, g + 1)
                    for c in range(G):
                        for k in range(KC):
                            last = nc.tensor.matmul(bank[0][c * 32:(c + 1) * 32, 0:N], wh_f[:, k, :], hT[:, k, c, :],
                                                    start=(k == 0), stop=(k == KC - 1))
                    last.then_inc(f_full, 1)

                def head(i):
                    if i == 0:
                        pe.wait_ge(agg_act, gm * 2 + 2)
                        pe.wait_ge(agg_dve, gm * 2 + 2)
                    for o in range(KC):
                        for k in range(KC):
                            last = nc.tensor.matmul(bank[3 + (6 + i) % 4][:, o * G * N:(o + 1) * G * N], wh[:, k, i, o * N:(o + 1) * N],
                                                    aggT[:, k, i].rearrange("p c n -> p (c n)"), start=(k == 0), stop=(k == KC - 1))
                    last.then_inc(hd2_full, 1)

                def out_product(c):
                    for i in range(H2):
                        pe.wait_ge(hd2_elu, gm * 8 + 2 * i + 2)
                        for o in range(KC):
                            k = i * KC + o
                            last = nc.tensor.matmul(bank[3 + (10 + c) % 4][:, 0:D + 2], headsT[:, i, o, c, :], wout[:, k, :],
                                                    start=(k == 0), stop=(k == H2 * KC - 1))
                    last.then_inc(wo2_full, 1)

                if m:
                    head(0)
                    head(1)
                if f:
                    pe.wait_ge(lr_step, g * 2 + 2)
                    if positive(g):
                        pe.wait_ge(scores2, g * 2)
                    for c in range(G):
                        nc.tensor.matmul(bank[1 + c][:, :], ident_bf[:, :], hide2[:, :, :], start=True, stop=False)
                    for c in range(G):
                        rows = slice(c * 32, (c + 1) * 32)
                        nc.tensor.matmul(bank[1 + c][:, :], left[rows, :], right[rows].rearrange("p h n -> p (h n)"),
                                         start=False, stop=True).then_inc(s2_full, 1)
                if l:
                    pe.wait_ge(p3_ready, gl + 1)
                    for c in range(G):
                        last = nc.tensor.transpose(bank[7][:, c * N:(c + 1) * N], t3[:, 0, c, :], ident)
                    last.then_inc(pT3_full, 1)
                if m:
                    head(2)
                    head(3)
                if l:
                    pe.wait_ge(pT3_ready, gl + 1)
                    for o in range(KC):
                        for c in range(G):
                            last = nc.tensor.matmul(bank[7][:, (o * G + c) * N:(o * G + c + 1) * N], wh2[:, c, o * N:(o + 1) * N],
                                                    p3T[:, c, :], start=True, stop=True)
                    last.then_inc(at3_full, 1)
                if m:
                    out_product(0)
                if l:
                    pe.wait_ge(at3_elu, gl * 2 + 2)
                    for o in range(KC):
                        for k in range(KC):
                            last = nc.tensor.matmul(bank[7][:, o * G * N:(o + 1) * G * N], ffn1[:, k, o * N:(o + 1) * N],
                                                    outT[:, k].rearrange("p c n -> p (c n)"), start=(k == 0), stop=(k == KC - 1))
                    last.then_inc(u_full, 1)
                if m:
                    out_product(1)
                if l:
                    pe.wait_ge(u_ready, gl + 1)
                    for c in range(G):
                        for k in range(KC):
                            nc.tensor.matmul(bank[7][:, c * D:(c + 1) * D], uT[:, k, c, :], ffn2[:, k, :], start=(k == 0), stop=False)
                        for k in range(KC):
                            last = nc.tensor.matmul(bank[7][:, c * D + k * N:c * D + (k + 1) * N], outT[:, k, c, :], ident,
                                                    start=False, stop=(k == KC - 1))
                    last.then_inc(y_full, 1)

            if PHASES > 2:
                pe.wait_ge(pre[1].x, NG)
                pe.wait_ge(late_setup, LATE_DONE)
                run_steps(pe, NG, step2)

            def step3(at):
                n, gn, pn = at.group(-1)
                f, g, p = at.group(0)
                m, gm, pm = at.group(1)
                l, gl, pl = at.group(2)
                if m:
                    pe.wait_ge(diag3, gm + 1)
                    if positive(gm):
                        pe.wait_ge(scores4, gm)
                    nc.tensor.matmul(bank[2][:, 0:G * N], ones[:, :], diag[:, pm].rearrange("p c n -> p (c n)"),
                                     start=True, stop=True).then_inc(s4_full, 1)
                if l:
                    pe.wait_ge(exp4, gl + 1)
                    if positive(gl):
                        pe.wait_ge(pT4_ready, gl)
                    for c in range(G):
                        last = nc.tensor.transpose(bank[3][:, c * N:(c + 1) * N], t3[:, pl, c, :], ident)
                    last.then_inc(pT4_full, 1)
                if f:
                    pe.wait_ge(hT3, g + 1)
                    if positive(g):
                        pe.wait_ge(h3_ready, g)
                    for c in range(G):
                        for k in range(KC):
                            last = nc.tensor.matmul(bank[1][:, c * (F3 + 2):(c + 1) * (F3 + 2)], hT[:, k, c, :], w3[:, k, :],
                                                    start=(k == 0), stop=(k == KC - 1))
                    last.then_inc(w3_full, 1)
                if l:
                    pe.wait_ge(pT4_ready, gl + 1)
                    if positive(gl):
                        pe.wait_ge(pre[3].x, gl)
                    for c in range(G):
                        last = nc.tensor.matmul(bank[4][:, c * F3:(c + 1) * F3], p3T[:, c, :], h3[:, at.quarter(2), c, 0:F3], start=True, stop=True)
                    last.then_inc(at4_full, 1)
                if n:
                    pe.wait_ge(pre[3].h, gn + 1)
                    if positive(gn):
                        pe.wait_ge(hT3, gn)
                    transpose_group(bank[0], h[:, pn]).then_inc(hT3_full, 1)

            if PHASES > 3:
                pe.wait_ge(pre[2].x, NG)
                run_steps(pe, NG, step3, 4)


def shape_constants():
    c = np.zeros((N, N + 4 + H2 * N), np.float32)
    c[:, :N] = np.eye(N)
    r = np.arange(N) % 32
    f1, f2 = r < H2, (r >= H2) & (r < 2 * H2)
    c[:, N], c[:, N + 1] = f1, f2
    c[:, N + 2], c[:, N + 3] = f2, f1
    for hh in range(H2):
        c[:, N + 4 + hh * N:N + 4 + (hh + 1) * N] = ((f1 | f2) & (r % H2 == hh))[:, None]
    return c


_INS = ['x', 'adj', 'L0_gnn_Wq', 'L0_gnn_bq', 'L0_gnn_Wk', 'L0_gnn_bk', 'L0_gnn_Wv', 'L0_gnn_bv', 'L0_gnn_Wo', 'L0_gnn_bo',
        'L1_gnn_W', 'L1_gnn_b', 'L2_gnn_W_heads', 'L2_gnn_a_heads', 'L2_gnn_W_out', 'L2_gnn_a_out', 'L2_gnn_w1', 'L2_gnn_b1',
        'L2_gnn_w2', 'L2_gnn_b2', 'L2_gnn_ln_gamma', 'L2_gnn_ln_beta', 'L3_gnn_W', 'L3_gnn_a']


def kernel(**inputs):
    import concourse.bacc as bacc
    from concourse.bass_utils import run_bass_kernel_spmd

    nc = bacc.Bacc("TRN2", target_bir_lowering=False, num_devices=1)
    arrays = {f"in_{name}": np.ascontiguousarray(inputs[name]) for name in _INS}
    for name in ('L0_gnn_bq', 'L0_gnn_bk', 'L0_gnn_bv', 'L2_gnn_b1'):
        arrays[f"in_{name}"] = np.ascontiguousarray(inputs[name].reshape(KC, N).T)
    arrays["in_shape_consts"] = shape_constants()
    args = [nc.dram_tensor(name, a.shape, mybir.dt.from_np(a.dtype), kind="ExternalInput").ap() for name, a in arrays.items()]
    out = nc.dram_tensor("out_x", arrays["in_x"].shape, FP32, kind="ExternalOutput").ap()
    build_program(nc, *args, out)
    return run_bass_kernel_spmd(nc, [arrays], core_ids=[0]).results[0]["out_x"]
```

```python
import numpy as np
import concourse.bass as bass
from concourse import mybir
from contextlib import ExitStack

FP32 = mybir.dt.float32
BF16 = mybir.dt.bfloat16
F32R = mybir.dt.float32r
INT32 = mybir.dt.int32
ALU = mybir.AluOpType
ACT = mybir.ActivationFunctionType
AX = mybir.AxisListType

N = 128
D = 256
KC = D // N
G = 2
H0, DH = 8, 32
H2 = 4
F3 = 128
LN_EPS = 1e-5
LEAK2, LEAK3 = 0.01, 0.2
NEG = -1e9
HIDE = -3e38
PHASES = 4


class Step:

    def __init__(self, t, phase, groups):
        self.t, self.phase, self.groups = t, phase, groups

    def group(self, lag):
        g = self.t - lag
        there = not isinstance(g, int) or 0 <= g < self.groups
        return there, g, (self.phase - lag) % 2

    def quarter(self, lag):
        return (self.phase - lag) % 4


def run_steps(eng, groups, step, turn=2, deepest=3):
    first = (deepest + turn) // turn * turn
    for t in range(-2, first):
        step(Step(t, t % turn, groups))
    with eng.Fori(first // turn, (groups - 2) // turn) as i:
        for u in range(turn):
            step(Step(i * turn + u, u, groups))
    for t in range((groups - 2) // turn * turn, groups + deepest):
        step(Step(t, t % turn, groups))


def positive(n):
    return not isinstance(n, int) or n > 0


def build_program(nc, x, adj, L0_gnn_Wq, L0_gnn_bq, L0_gnn_Wk, L0_gnn_bk, L0_gnn_Wv, L0_gnn_bv, L0_gnn_Wo,
                  L0_gnn_bo, L1_gnn_W, L1_gnn_b, L2_gnn_W_heads, L2_gnn_a_heads, L2_gnn_W_out, L2_gnn_a_out,
                  L2_gnn_w1, L2_gnn_b1, L2_gnn_w2, L2_gnn_b2, L2_gnn_ln_gamma, L2_gnn_ln_beta, L3_gnn_W,
                  L3_gnn_a, shape_consts, out):
    B = x.shape[0]
    NG = B // G
    GD = G * D
    x_d = x.rearrange("b n d -> n b d")
    out_d = out.rearrange("b n d -> n b d")

    ctx = ExitStack()
    with ctx:
        def sb(name, shape, dt=FP32):
            return ctx.enter_context(nc.sbuf_tensor(name, shape, dt))

        def sem(name):
            return ctx.enter_context(nc.semaphore(name))

        x_all = sb("x_all", [N, B, D])
        wh_f = sb("wh_f", [N, KC, DH])
        ffn1 = sb("ffn1", [N, KC, D])
        ffn2 = sb("ffn2", [N, KC, D])
        w3 = sb("w3", [N, KC, F3 + 2])
        consts = sb("consts", [N, N + 4 + H2 * N])
        ident = consts[:, 0:N]
        left_mul, left_add = consts[:, N:N + 1], consts[:, N + 1:N + 2]
        right_mul, right_add = consts[:, N + 2:N + 3], consts[:, N + 3:N + 4]
        head_rows = consts[:, N + 4:].rearrange("p (h n) -> p h n", h=H2)
        ident_bf = sb("ident_bf", [N, N], BF16)
        ones = sb("ones", [N, N])
        adj_i = sb("adj_i", [N, N], INT32)
        adj_f = sb("adj_f", [N, N])
        adjT = sb("adjT", [N, N])
        hide0 = sb("hide0", [N, 4, N], BF16)
        hide2 = sb("hide2", [N, 4, N], BF16)
        neg3 = sb("neg3", [N, N])
        edge = sb("edge", [N, N])
        deg = sb("deg", [N, 1])
        edges = sb("edges", [N, 1])
        poison = sb("poison", [N, 1])
        bq_c = sb("bq_c", [N, KC])
        bk_c = sb("bk_c", [N, KC])
        bv_c = sb("bv_c", [N, KC])
        b1_c = sb("b1_c", [N, KC])
        bv_wide = sb("bv_wide", [N, KC, N])
        bo_row = sb("bo_row", [N, 1, D])
        degb_row = sb("degb_row", [N, 1, D])
        b2_row = sb("b2_row", [N, 1, D])
        gamma_row = sb("gamma_row", [N, 1, D])
        beta_row = sb("beta_row", [N, 1, D])
        pow_half = sb("pow_half", [N, G])
        eps_tile = sb("eps_tile", [N, G])
        minus_one = sb("minus_one", [N, G])

        st = sb("st", [N, 2, G, 6])
        mv = sb("mv", [N, 2, G, 2])
        var_eps = sb("var_eps", [N, 2, G])
        rstd = sb("rstd", [N, 2, G])
        mean_rstd = sb("mean_rstd", [N, 2, G])
        shift = sb("shift", [N, 2, G])
        h = sb("h", [N, 2, G, D])
        hT = sb("hT", [N, KC, G, N])

        probs = sb("probs", [N, 4, 4, N])
        probsT = sb("probsT", [N, 4, 4, N])
        top0 = sb("top0", [N, 4, 4])
        rsum0 = sb("rsum0", [N, G, H0])

        left = sb("left", [64, N])
        right_rows = sb("right_rows", [64, N])
        right = sb("right", [64, H2, N])
        negtop2 = sb("negtop2", [N, G, H2])
        sum2 = sb("sum2", [N, G, H2])
        rsum2 = sb("rsum2", [N, G, H2])
        em = sb("em", [N, 2, KC, GD // 2])
        wh2 = sb("wh2", [N, 2, G, D + 2])
        diag = sb("diag", [N, 2, G, N])
        t3 = sb("t3", [N, 2, G, N])
        negtop = sb("negtop", [N, G])
        sum3 = sb("sum3", [N, 2, G])
        rsum3 = sb("rsum3", [N, G])
        p3T = sb("p3T", [N, G, N])
        em3 = sb("em3", [N, KC, G, N])
        outT = sb("outT", [N, KC, G, N])
        uT = sb("uT", [N, KC, G, N])
        y = sb("y", [N, G, D])
        st_y = sb("st_y", [N, G, 6])
        mv_y = sb("mv_y", [N, G, 2])
        var_y = sb("var_y", [N, G])
        rstd_y = sb("rstd_y", [N, G])
        h3 = sb("h3", [N, 4, G, F3 + 2])

        def taker(stack):
            return lambda name, shape, dt=FP32: stack.enter_context(nc.sbuf_tensor(name, shape, dt))

        with ExitStack() as early:
            sb_early = taker(early)
            raw1 = sb_early("raw1", [N, KC, 2 * D])
            a_heads = sb_early("a_heads", [N, H2 * 2 * D])
            wh = sb_early("wh", [N, KC, H2, D])
            wout = sb_early("wout", [N, H2 * KC, D + 2])
            prod = sb_early("prod", [N, H2 * D])
            with ExitStack() as layer0:
                sb_0 = taker(layer0)
                wqT_hi, wqT_lo, wkT_hi, wkT_lo, wvT_hi, wvT_lo = [
                    sb_0(f"w{w}T_{part}", [N, KC, D], F32R) for w in "qkv" for part in ("hi", "lo")]
                woT = sb_0("woT", [N, KC, D])
                hT_hi = sb_0("hT_hi", [N, KC, G, N], F32R)
                hT_lo = sb_0("hT_lo", [N, KC, G, N], F32R)
                qT = sb_0("qT", [N, KC, G, N])
                kT = sb_0("kT", [N, KC, G, N])
                v1 = sb_0("v1", [N, 2, G, H0, DH + 1])
                att0 = sb_0("att0", [N, G, H0, DH])
                att0T = sb_0("att0T", [N, KC, G, N])
            with ExitStack() as layer1:
                sb_1 = taker(layer1)
                w1T_hi = sb_1("w1T_hi", [N, 2 * KC, D], F32R)
                w1T_lo = sb_1("w1T_lo", [N, 2 * KC, D], F32R)
                hd = sb_1("hd", [N, 2, G, D])
                hdT_hi, hdT_lo, ahT_hi, ahT_lo = [sb_1(name, [N, 2, KC, G, N], F32R) for name in ("hdT_hi", "hdT_lo", "ahT_hi", "ahT_lo")]
        aggT_hi = sb("aggT_hi", [N, KC, H2, G, N], F32R)
        aggT_lo = sb("aggT_lo", [N, KC, H2, G, N], F32R)
        headsT_hi = sb("headsT_hi", [N, H2, KC, G, N], F32R)
        headsT_lo = sb("headsT_lo", [N, H2, KC, G, N], F32R)
        wh_hi = sb("wh_hi", [N, KC, H2, D], F32R)
        wh_lo = sb("wh_lo", [N, KC, H2, D], F32R)
        wout_hi = sb("wout_hi", [N, H2 * KC, D + 2], F32R)
        wout_lo = sb("wout_lo", [N, H2 * KC, D + 2], F32R)

        bank = [ctx.enter_context(nc.psum_tensor(f"bank{i}", [N, 512], FP32)) for i in range(8)]
        raw = probsT[:, :, :, :].rearrange("p a b n -> p (a b n)").rearrange("p (w c d) -> p w c d", w=4, c=2)
        a_heads_rows = a_heads[:, :]
        a_out_rows = em[:, 0, :, :].rearrange("p c n -> p (c n)")[:, 0:2 * D].rearrange("p (s d) -> p s d", s=2)
        a3_rows = h3[:, 0, :, 0:F3]

        loads_done = sem("loads_done")
        later_loads_done = sem("later_loads_done")
        x_loaded = [sem("x_loaded0"), sem("x_loaded1")]
        pool_setup = sem("pool_setup")
        dve_setup = sem("dve_setup")
        weights_T = sem("weights_T")
        weights_dve = sem("weights_dve")
        weights_act = sem("weights_act")
        late_setup = sem("late_setup")
        out_stored = sem("out_stored")

        class Pre:
            def __init__(self, k):
                self.stats = sem(f"stats{k}")
                self.norm = sem(f"norm{k}")
                self.h = sem(f"h{k}")
                self.bias = sem(f"bias{k}")
                self.x = sem(f"x_done{k}")

        pre = [Pre(k) for k in range(4)]

        def pre_dve(dve, k, at):
            there, g, p = at.group(-2)
            if not there:
                return
            s = pre[k]
            if k == 0:
                dve.wait_ge(x_loaded[p], (g - p) * 8 + 16)
            for c in range(G):
                last = nc.vector.bn_stats(st[:, p, c, :], x_all[:, bass.ds(g * G + c, 1), :].rearrange("p a d -> p (a d)"))
            last.then_inc(s.stats, 1)

        def stats_written(dve, k, at):
            there, g, p = at.group(-2)
            if there:
                dve.wait_ge(pre[k].stats, g * 2 + 1)

        def moments_dve(k, at):
            there, g, p = at.group(-2)
            if not there:
                return
            s = pre[k]
            for c in range(G):
                last = nc.vector.bn_aggr(mv[:, p, c, :], st[:, p, c, :])
            last.then_inc(s.stats, 1)

        def pre_pool(pool, k, at):
            there, g, p = at.group(-2)
            if not there:
                return
            s = pre[k]
            pool.wait_ge(s.stats, g * 2 + 2)
            if positive(g - 1):
                pool.wait_ge(s.h, g - 1)
            nc.gpsimd.tensor_tensor(var_eps[:, p, :], mv[:, p, :, 1], eps_tile[:, :], ALU.add).then_inc(s.norm, 1)
            pool.wait_ge(s.norm, g * 4 + 1)
            nc.gpsimd.tensor_tensor(rstd[:, p, :], var_eps[:, p, :], pow_half[:, :], ALU.pow).then_inc(s.norm, 1)
            pool.wait_ge(s.norm, g * 4 + 2)
            nc.gpsimd.tensor_tensor(mean_rstd[:, p, :], mv[:, p, :, 0], rstd[:, p, :], ALU.mult).then_inc(s.norm, 1)
            pool.wait_ge(s.norm, g * 4 + 3)
            nc.gpsimd.tensor_tensor(shift[:, p, :], mean_rstd[:, p, :], minus_one[:, :], ALU.mult).then_inc(s.norm, 1)

        def pre_act(act, k, at):
            there, g, p = at.group(-1)
            if not there:
                return
            s = pre[k]
            act.wait_ge(s.norm, g * 4 + 4)
            for c in range(G):
                last = nc.scalar.activation(h[:, p, c, :], x_all[:, bass.ds(g * G + c, 1), :].rearrange("p a d -> p (a d)"),
                                            ACT.Relu, bias=shift[:, p, c:c + 1], scale=rstd[:, p, c:c + 1])
            last.then_inc(s.h, 1)

        def x_group(g):
            return x_all[:, bass.ds(g * G, G), :]

        def bias_pool(pool, k, at, row):
            there, g, p = at.group(0)
            if not there:
                return
            pool.wait_ge(pre[k].h, g + 1)
            nc.gpsimd.tensor_tensor(x_group(g), x_group(g), row[:, :, :].broadcast_to([N, G, D]), ALU.add).then_inc(pre[k].bias, 1)

        hT0_hi = sem("hT0_hi")
        hT0_lo = sem("hT0_lo")
        hT0_full = sem("hT0_full")
        q_full = sem("q_full")
        k_full = sem("k_full")
        v_full = sem("v_full")
        q_ready = sem("q_ready")
        k_ready = sem("k_ready")
        v_ready = sem("v_ready")
        s0_full = sem("s0_full")
        top0_ready = sem("top0_ready")
        s0_sub = sem("s0_sub")
        p0_ready = sem("p0_ready")
        pT0_full = sem("pT0_full")
        pT0_act = sem("pT0_act")
        pT0_dve = sem("pT0_dve")
        av_full = sem("av_full")
        rsum0_step = sem("rsum0_step")
        att0_ready = sem("att0_ready")
        aT_full = sem("aT_full")
        aT_ready = sem("aT_ready")
        o_full = sem("o_full")
        hd_ready = sem("hd_ready")
        hdT_full = sem("hdT_full")
        w1_lo = sem("w1_lo")
        hdT_ready = [sem("hdT_hi_ready"), sem("hdT_lo_ready")]
        ahT_full = sem("ahT_full")
        ahT_ready = [sem("ahT_hi_ready"), sem("ahT_lo_ready")]
        o1_full = sem("o1_full")
        hT2_full = sem("hT2_full")
        hT2 = sem("hT2")
        f_full = sem("f_full")
        lr_step = sem("lr_step")
        s2_full = sem("s2_full")
        scores2 = sem("scores2")
        soft2 = sem("soft2")
        soft2n = sem("soft2n")
        exp2 = sem("exp2")
        pT2_full = sem("pT2_full")
        pT2_ready = sem("pT2_ready")
        w_hi = sem("w_hi")
        w_lo = sem("w_lo")
        agg_full = sem("agg_full")
        agg_hi = sem("agg_hi")
        agg_lo = sem("agg_lo")
        hd2_full = sem("hd2_full")
        hd2_exp = sem("hd2_exp")
        hd2_elu = sem("hd2_elu")
        hd2_hi = sem("hd2_hi")
        hd2_lo = sem("hd2_lo")
        wo2_full = sem("wo2_full")
        wh2_act = sem("wh2_act")
        wh2_dve = sem("wh2_dve")
        diag2 = sem("diag2")
        s3_full = sem("s3_full")
        scores3 = sem("scores3")
        top3 = sem("top3")
        exp3 = sem("exp3")
        rsum3_ready = sem("rsum3_ready")
        p3_ready = sem("p3_ready")
        pT3_full = sem("pT3_full")
        pT3_ready = sem("pT3_ready")
        at3_full = sem("at3_full")
        at3_exp = sem("at3_exp")
        at3_elu = sem("at3_elu")
        u_full = sem("u_full")
        u_ready = sem("u_ready")
        y_full = sem("y_full")
        y_step = sem("y_step")
        y_norm = sem("y_norm")
        yn_ready = sem("yn_ready")
        yg_ready = sem("yg_ready")
        hT3_full = sem("hT3_full")
        hT3 = sem("hT3")
        w3_full = sem("w3_full")
        h3_ready = sem("h3_ready")
        diag3 = sem("diag3")
        s4_full = sem("s4_full")
        scores4 = sem("scores4")
        soft4 = sem("soft4")
        exp4 = sem("exp4")
        pT4_full = sem("pT4_full")
        pT4_ready = sem("pT4_ready")
        at4_full = sem("at4_full")
        rsum4 = sem("rsum4")

        def flat(t):
            return t[:, :, :, :].rearrange("p a b c -> p (a b c)") if len(t.shape) == 4 else t[:, :, :].rearrange("p a b -> p (a b)")

        block = ctx.enter_context(nc.Block())

        FIRST_LOADS, LATER_LOADS = [], []

        def load(dst, src):
            FIRST_LOADS.append((dst, src))

        load(consts[:, :], shape_consts)
        load(adj_i[:, :], adj)
        for i, w in enumerate((L0_gnn_Wq, L0_gnn_Wk, L0_gnn_Wv, L0_gnn_Wo)):
            load(raw[:, i], w.rearrange("(c p) d -> p c d", p=N))
        for dst, src in ((bq_c, L0_gnn_bq), (bk_c, L0_gnn_bk), (bv_c, L0_gnn_bv), (b1_c, L2_gnn_b1)):
            load(dst[:, :], src)
        load(bo_row[:, 0, :], L0_gnn_bo.partition_broadcast(N))

        def load(dst, src):
            LATER_LOADS.append((dst, src))

        load(raw1[:, :, :], L1_gnn_W.rearrange("(c p) e -> p c e", p=N))
        for dst, src in ((degb_row, L1_gnn_b), (b2_row, L2_gnn_b2),
                         (gamma_row, L2_gnn_ln_gamma), (beta_row, L2_gnn_ln_beta)):
            load(dst[:, 0, :], src.partition_broadcast(N))
        for c in range(KC):
            load(wh[:, c], L2_gnn_W_heads.rearrange("h (c p) o -> p c h o", p=N)[:, c])
        load(a_heads_rows, L2_gnn_a_heads.rearrange("h s -> (h s)").partition_broadcast(N))
        load(wout[:, :, 0:D], L2_gnn_W_out.rearrange("(k p) o -> p k o", p=N))
        load(a_out_rows, L2_gnn_a_out.rearrange("(s d) -> s d", s=2).partition_broadcast(N))
        load(ffn1[:, :, :], L2_gnn_w1.rearrange("(c p) o -> p c o", p=N))
        load(ffn2[:, :, :], L2_gnn_w2.rearrange("(c p) o -> p c o", p=N))
        load(w3[:, :, 0:F3], L3_gnn_W.rearrange("(c p) o -> p c o", p=N))
        load(a3_rows, L3_gnn_a.rearrange("s o e -> s (o e)").partition_broadcast(N))
        LOADED, LATER_LOADED = 16 * len(FIRST_LOADS), 16 * len(LATER_LOADS)

        MASKS_DONE, BV_DONE = 4, 6
        BO_DONE = BV_DONE + 1
        LATE_DONE = 4 + 4 * H2 + 8 + 4

        @block.sync
        def _(sp):
            for dst, src in FIRST_LOADS:
                sp.dma_start(dst, src).then_inc(loads_done, 16)
            for g in range(2):
                sp.dma_start(x_group(g), x_d[:, g * G:(g + 1) * G, :]).then_inc(x_loaded[g], 16)
            for dst, src in LATER_LOADS:
                sp.dma_start(dst, src).then_inc(later_loads_done, 16)
            with sp.Fori(1, NG // 2) as i:
                for p in range(2):
                    sp.wait_ge(x_loaded[p], i * 16)
                    sp.dma_start(x_group(i * 2 + p), x_d[:, bass.ds((i * 2 + p) * G, G), :]).then_inc(x_loaded[p], 16)
            with sp.Fori(0, NG) as g:
                sp.wait_ge(pre[PHASES - 1].x, g + 1)
                sp.dma_start(out_d[:, bass.ds(g * G, G), :], x_group(g)).then_inc(out_stored, 16)
            sp.wait_ge(out_stored, NG * 16)

        @block.gpsimd
        def _(pool):
            nc.gpsimd.memset(pow_half[:, :], -0.5)
            nc.gpsimd.memset(eps_tile[:, :], LN_EPS)
            nc.gpsimd.memset(minus_one[:, :], -1.0)
            nc.gpsimd.memset(ones[:, :], 1.0)
            nc.gpsimd.memset(v1[:, :, :, :, :], 1.0)
            nc.gpsimd.memset(wh_f[:, :, :], 0.0).then_inc(pool_setup, 1)
            pool.wait_ge(pool_setup, 1)

            pool.wait_ge(dve_setup, BO_DONE)

            def step0(at):
                bias_pool(pool, 0, at, bo_row)
                pre_pool(pool, 0, at)

            run_steps(pool, NG, step0)
            if PHASES > 1:
                pool.wait_ge(pre[0].x, NG)
                pool.wait_ge(late_setup, LATE_DONE)

                def step1(at):
                    bias_pool(pool, 1, at, degb_row)
                    pre_pool(pool, 1, at)

                run_steps(pool, NG, step1)
            if PHASES > 2:
                pool.wait_ge(pre[1].x, NG)

                def step2(at):
                    there, g, p = at.group(4)
                    if there:
                        pool.wait_ge(y_step, g * 3 + 3)
                        nc.gpsimd.tensor_tensor(var_y[:, :], mv_y[:, :, 1], eps_tile[:, :], ALU.add).then_inc(y_norm, 1)
                        pool.wait_ge(y_norm, g * 2 + 1)
                        nc.gpsimd.tensor_tensor(rstd_y[:, :], var_y[:, :], pow_half[:, :], ALU.pow).then_inc(y_norm, 1)
                    bias_pool(pool, 2, at, beta_row)
                    pre_pool(pool, 2, at)
                    if there:
                        pool.wait_ge(yn_ready, g + 1)
                        nc.gpsimd.tensor_tensor(y[:, :], y[:, :], gamma_row[:, :, :].broadcast_to([N, G, D]),
                                                ALU.mult).then_inc(yg_ready, 1)
                        pool.wait_ge(yg_ready, g + 1)
                        nc.gpsimd.tensor_tensor(x_group(g), x_group(g), y[:, :], ALU.add).then_inc(pre[2].x, 1)

                run_steps(pool, NG, step2, deepest=4)
            if PHASES > 3:
                pool.wait_ge(pre[2].x, NG)
                run_steps(pool, NG, lambda at: pre_pool(pool, 3, at), 4)


        @block.vector
        def _(dve):
            count = [0]

            def link(ins):
                count[0] += 1
                ins.then_inc(dve_setup, 1)
                dve.wait_ge(dve_setup, count[0])

            dve.wait_ge(loads_done, LOADED)
            dve.wait_ge(pool_setup, 1)
            link(nc.vector.tensor_copy(adj_f[:, :], adj_i[:, :]))
            nc.vector.tensor_copy(ident_bf[:, :], ident)
            for i in range(4):
                nc.vector.tensor_scalar(hide0[:, i, :], adj_f[:, :], 0.0, HIDE, ALU.is_equal, ALU.mult)
            link(nc.vector.tensor_scalar(edge[:, :], adj_f[:, :], 0.0, 0.0, ALU.not_equal, ALU.add, accum_out=edges[:, :]))
            link(nc.vector.reciprocal(poison[:, :], edges[:, :]))
            link(nc.vector.tensor_scalar(poison[:, :], poison[:, :], 0.0, None, ALU.mult))
            assert count[0] == MASKS_DONE
            for c in range(KC):
                link(nc.vector.tensor_scalar(bv_wide[:, c, :], ones[:, :], bv_c[:, c:c + 1], None, ALU.mult))
            assert count[0] == BV_DONE
            for i, dst in ((1, wkT_hi), (3, woT)):
                dve.wait_ge(weights_T, i + 1)
                nc.vector.tensor_copy(dst[:, :, :], bank[i][:, :].rearrange("p (c o) -> p c o", c=2)).then_inc(weights_dve, 1)
            dve.wait_ge(weights_act, 2)
            dve.wait_ge(weights_dve, 1)
            for i, lo, hi in ((0, wqT_lo, wqT_hi), (1, wkT_lo, wkT_hi), (2, wvT_lo, wvT_hi)):
                nc.vector.tensor_tensor(lo[:, :, :], bank[i][:, :].rearrange("p (c o) -> p c o", c=2), hi[:, :, :].bitcast(FP32),
                                        ALU.subtract).then_inc(weights_dve, 1)
            dve.wait_ge(weights_T, 5)
            link(nc.vector.tensor_tensor(bo_row[:, 0, :], bank[7][:, 0:D], bo_row[:, 0, :], ALU.add))
            assert count[0] == BO_DONE

            prod4 = prod[:, 0:KC * D].rearrange("p (c o) -> p c o", c=KC)
            prod8 = prod[:, :].rearrange("p (k o) -> p k o", k=H2)
            prod3 = prod[:, 0:KC * F3].rearrange("p (c o) -> p c o", c=KC)
            av = a_heads_rows.rearrange("p (h s o) -> p h s o", h=H2, s=2)
            late_count = [0]

            def late(ins):
                late_count[0] += 1
                ins.then_inc(late_setup, 1)
                dve.wait_ge(late_setup, late_count[0])

            def late_part(i):
                if i == 0:
                    dve.wait_ge(later_loads_done, LATER_LOADED)
                    for k in range(4):
                        nc.vector.tensor_scalar(hide2[:, k, :], adj_f[:, :], 0.0, HIDE, ALU.is_le, ALU.mult)
                    late(nc.vector.reduce_sum(deg[:, :], adj_f[:, :], AX.X))
                    late(nc.vector.tensor_scalar(degb_row[:, 0, :], degb_row[:, 0, :], deg[:, :], None, ALU.mult))
                    late(nc.vector.tensor_scalar(neg3[:, :], adj_f[:, :], -1.0, 1.0, ALU.mult, ALU.add))
                    late(nc.vector.tensor_scalar(neg3[:, :], neg3[:, :], NEG, None, ALU.mult))
                if i in (1, 2):
                    s = i - 1
                    for hh in range(H2):
                        late(nc.vector.tensor_tensor(prod4, wh[:, :, hh, :], av[:, hh, s:s + 1, :].broadcast_to([N, KC, D]), ALU.mult))
                        late(nc.vector.reduce_sum(wh_f[:, :, s * H2 + hh], prod4, AX.X))
                if i in (0, 3):
                    s = i // 3
                    for k in (slice(0, H2), slice(H2, H2 * KC)):
                        late(nc.vector.tensor_tensor(prod8, wout[:, k, 0:D], a_out_rows[:, s:s + 1, :].broadcast_to([N, H2, D]), ALU.mult))
                        late(nc.vector.reduce_sum(wout[:, k, D + s], prod8, AX.X))
                if i == 3:
                    for s in range(2):
                        late(nc.vector.tensor_tensor(prod3, w3[:, :, 0:F3], a3_rows[:, s:s + 1, :].broadcast_to([N, KC, F3]), ALU.mult))
                        late(nc.vector.reduce_sum(w3[:, :, F3 + s], prod3, AX.X))

            def step0(at):
                f, g, p = at.group(0)
                b, gb, pb = at.group(1)
                def probs_T(r):
                    dve.wait_ge(pT0_full, gb * 4 + r + 1)
                    if positive(gb) and r == 1:
                        dve.wait_ge(av_full, gb * 2)
                    nc.vector.tensor_copy(probsT[:, r], bank[3][:, :].rearrange("p (k n) -> p k n", k=4)).then_inc(pT0_dve, 1)

                if b:
                    probs_T(1)
                if f:
                    dve.wait_ge(k_full, g + 1)
                    if positive(g):
                        dve.wait_ge(s0_full, g * 4)
                    for c in range(KC):
                        last = nc.vector.tensor_scalar(kT[:, c], bank[0][:, c * 256:(c + 1) * 256].rearrange("p (c n) -> p c n", c=G),
                                                       bk_c[:, c:c + 1], None, ALU.add)
                    last.then_inc(k_ready, 1)
                if b:
                    probs_T(3)
                pre_dve(dve, 0, at)
                if not b:
                    stats_written(dve, 0, at)
                    moments_dve(0, at)
                if b:
                    dve.wait_ge(av_full, gb * 2 + 2)
                    stats_written(dve, 0, at)
                    for c in range(G):
                        o = bank[2 + c][:, 0:H0 * (DH + 1)].rearrange("p (h e) -> p h e", h=H0)
                        last = nc.vector.reciprocal(rsum0[:, c, :], o[:, :, DH])
                    last.then_inc(rsum0_step, 1)
                    moments_dve(0, at)
                    dve.wait_ge(rsum0_step, gb * 2 + 1)
                    nc.vector.tensor_scalar(rsum0[:, :, :], rsum0[:, :, :], poison[:, :], None, ALU.add).then_inc(rsum0_step, 1)
                    dve.wait_ge(rsum0_step, gb * 2 + 2)
                    if positive(gb):
                        dve.wait_ge(aT_full, gb)
                    for c in range(G):
                        o = bank[2 + c][:, 0:H0 * (DH + 1)].rearrange("p (h e) -> p h e", h=H0)
                        last = nc.vector.tensor_tensor(att0[:, c], o[:, :, 0:DH],
                                                       rsum0[:, c, :].unsqueeze(2).broadcast_to([N, H0, DH]), ALU.mult)
                    last.then_inc(att0_ready, 1)
                n, gn, _ = at.group(-1)
                if n:
                    dve.wait_ge(hT0_hi, gn + 1)
                    nc.vector.tensor_tensor(hT_lo[:, :, :, :], bank[0][:, :].rearrange("p (k c n) -> p k c n", k=KC, c=G),
                                            hT_hi[:, :, :, :].bitcast(FP32), ALU.subtract).then_inc(hT0_lo, 1)

                def less_top(u):
                    for r in (2 * u, 2 * u + 1):
                        dve.wait_ge(s0_full, g * 4 + r + 1)
                        last = nc.vector.reduce_max(top0[:, r, :], bank[4 + r][:, :].rearrange("p (k n) -> p k n", k=4), AX.X)
                    last.then_inc(top0_ready, 1)
                    dve.wait_ge(top0_ready, g * 2 + u + 1)
                    if positive(g) and u == 0:
                        dve.wait_ge(pT0_full, g * 4)
                    for r in (2 * u, 2 * u + 1):
                        last = nc.vector.tensor_tensor(probs[:, r], bank[4 + r][:, :].rearrange("p (k n) -> p k n", k=4),
                                                       top0[:, r, :].unsqueeze(2).broadcast_to([N, 4, N]), ALU.subtract)
                    last.then_inc(s0_sub, 1)

                if f:
                    less_top(0)
                if b:
                    dve.wait_ge(o_full, gb + 1)
                    dve.wait_ge(pre[0].bias, gb + 1)
                    nc.vector.tensor_tensor(x_group(gb), bank[3][:, :].rearrange("p (c d) -> p c d", c=G), x_group(gb),
                                            ALU.add).then_inc(pre[0].x, 1)
                if f:
                    less_top(1)
                if isinstance(at.t, int) and 0 <= at.t < 4:
                    late_part(at.t)

            run_steps(dve, NG, step0)
            assert late_count[0] == LATE_DONE

            def step1(at):
                pre_dve(dve, 1, at)
                f, g, p = at.group(0)
                b, gb, pb = at.group(1)
                stats_written(dve, 1, at)
                if f:
                    for ready, hi, lo, b0 in ((hdT_ready, hdT_hi, hdT_lo, 0), (ahT_ready, ahT_hi, ahT_lo, 2)):
                        dve.wait_ge(ready[0], g + 1)
                        nc.vector.tensor_tensor(lo[:, p], bank[b0 + p][:, :].rearrange("p (k c n) -> p k c n", k=KC, c=G),
                                                hi[:, p].bitcast(FP32), ALU.subtract).then_inc(ready[1], 1)
                moments_dve(1, at)
                n, gn, pn = at.group(-1)
                if n:
                    dve.wait_ge(pre[1].h, gn + 1)
                    if positive(gn - 1):
                        dve.wait_ge(hdT_full, gn - 1)
                    nc.vector.tensor_scalar(hd[:, pn], h[:, pn], deg[:, :], None, ALU.mult).then_inc(hd_ready, 1)
                if b:
                    dve.wait_ge(o1_full, gb + 1)
                    dve.wait_ge(pre[1].bias, gb + 1)
                    nc.vector.tensor_tensor(x_group(gb), bank[4 + pb][:, :].rearrange("p (c d) -> p c d", c=G), x_group(gb),
                                            ALU.add).then_inc(pre[1].x, 1)

            if PHASES > 1:
                dve.wait_ge(pre[0].x, NG)
                for i in range(2):
                    dve.wait_ge(weights_act, 4 + i)
                    nc.vector.tensor_tensor(w1T_lo[:, i * 2:i * 2 + 2, :], bank[4 + i][:, :].rearrange("p (c o) -> p c o", c=2),
                                            w1T_hi[:, i * 2:i * 2 + 2, :].bitcast(FP32), ALU.subtract).then_inc(w1_lo, 1)
                run_steps(dve, NG, step1)

            def step2(at):
                f, g, p = at.group(0)
                m, gm, pm = at.group(1)
                o2, go, po = at.group(2)
                l, gl, pl = at.group(3)
                e, ge, pe_ = at.group(4)

                def elu_head(i):
                    dve.wait_ge(hd2_exp, gm * 4 + i + 1)
                    nc.vector.tensor_scalar(em[:, i % 2], em[:, i % 2], 1.0, -1.0, ALU.min, ALU.add).then_inc(hd2_elu, 1)
                    dve.wait_ge(hd2_elu, gm * 8 + 2 * i + 1)
                    nc.vector.tensor_tensor(em[:, i % 2], bank[3 + i % 2][:, :].rearrange("p (k n) -> p k n", k=KC), em[:, i % 2],
                                            ALU.max).then_inc(hd2_elu, 1)

                def low_head(i, gm):
                    dve.wait_ge(hd2_hi, gm * 4 + i + 1)
                    nc.vector.tensor_tensor(headsT_lo[:, i].rearrange("p k c n -> p k (c n)"), em[:, i % 2],
                                            headsT_hi[:, i].rearrange("p k c n -> p k (c n)").bitcast(FP32), ALU.subtract).then_inc(hd2_lo, 1)

                def low_agg(i):
                    dve.wait_ge(agg_hi, gm * 4 + i + 1)
                    c, dc = i // 2, i % 2
                    nc.vector.tensor_tensor(aggT_lo[:, dc, :, c, :], bank[3 + (2 + i) % 4][:, :].rearrange("p (h n) -> p h n", h=H2),
                                            aggT_hi[:, dc, :, c, :].bitcast(FP32), ALU.subtract).then_inc(agg_lo, 1)

                def soft(c):
                    dve.wait_ge(scores2, g * 2 + c + 1)
                    nc.vector.scalar_tensor_tensor(probs[:, c], probs[:, c], LEAK2, probs[:, c], ALU.mult, ALU.max).then_inc(soft2, 1)
                    dve.wait_ge(soft2, g * 4 + c * 2 + 1)
                    nc.vector.tensor_reduce(negtop2[:, c, :], probs[:, c], AX.X, ALU.max, negate=True).then_inc(soft2, 1)

                def normalise(c):
                    dve.wait_ge(exp2, g * 2 + c + 1)
                    nc.vector.reciprocal(rsum2[:, c, :], sum2[:, c, :]).then_inc(soft2n, 1)
                    dve.wait_ge(soft2n, g * 4 + c * 2 + 1)
                    nc.vector.tensor_tensor(probs[:, c], probs[:, c], rsum2[:, c, :].unsqueeze(2).broadcast_to([N, H2, N]),
                                            ALU.mult).then_inc(soft2n, 1)

                if f:
                    dve.wait_ge(hT2_full, g + 1)
                    if positive(g):
                        dve.wait_ge(f_full, g)
                    nc.vector.tensor_copy(hT[:, :, :, :], bank[0][:, :].rearrange("p (k c n) -> p k c n", k=KC, c=G)).then_inc(hT2, 1)
                if f:
                    dve.wait_ge(f_full, g + 1)
                    if positive(g):
                        dve.wait_ge(s2_full, g * 2)
                    nc.vector.tensor_scalar(left[:, :], bank[0][0:64, 0:N], left_mul[0:64], left_add[0:64], ALU.mult, ALU.add)
                    nc.vector.tensor_scalar(right_rows[:, :], bank[0][0:64, 0:N], right_mul[0:64], right_add[0:64],
                                            ALU.mult, ALU.add).then_inc(lr_step, 1)
                    dve.wait_ge(lr_step, g * 2 + 1)
                    nc.vector.tensor_tensor(right[:, :, :], right_rows[:, :].unsqueeze(1).broadcast_to([64, H2, N]),
                                            head_rows[0:64], ALU.mult).then_inc(lr_step, 1)
                if o2:
                    low_head(3, go)
                if m:
                    low_agg(0)
                if e:
                    dve.wait_ge(y_full, ge + 1)
                    if positive(ge):
                        dve.wait_ge(pre[2].x, ge)
                    nc.vector.tensor_tensor(y[:, :], bank[7][:, :].rearrange("p (c d) -> p c d", c=G),
                                            b2_row[:, :, :].broadcast_to([N, G, D]), ALU.add).then_inc(y_step, 1)
                if m:
                    low_agg(1)
                if e:
                    dve.wait_ge(y_step, ge * 3 + 1)
                    for c in range(G):
                        last = nc.vector.bn_stats(st_y[:, c, :], y[:, c, :])
                    last.then_inc(y_step, 1)
                if e:
                    dve.wait_ge(y_step, ge * 3 + 2)
                if f:
                    soft(0)
                if e:
                    for c in range(G):
                        last = nc.vector.bn_aggr(mv_y[:, c, :], st_y[:, c, :])
                    last.then_inc(y_step, 1)
                if m:
                    low_agg(2)
                if f:
                    soft(1)
                if m:
                    low_agg(3)
                if l:
                    dve.wait_ge(scores3, gl + 1)
                    nc.vector.scalar_tensor_tensor(t3[:, 0], t3[:, 0], LEAK2, t3[:, 0], ALU.mult, ALU.max).then_inc(top3, 1)
                    dve.wait_ge(top3, gl * 2 + 1)
                    nc.vector.tensor_reduce(negtop[:, :], t3[:, 0], AX.X, ALU.max, negate=True).then_inc(top3, 1)
                pre_dve(dve, 2, at)
                stats_written(dve, 2, at)
                if l:
                    dve.wait_ge(exp3, gl + 1)
                    nc.vector.reciprocal(rsum3[:, :], sum3[:, 0, :]).then_inc(rsum3_ready, 1)
                    dve.wait_ge(rsum3_ready, gl + 1)
                    for c in range(G):
                        last = nc.vector.tensor_scalar(t3[:, 0, c, :], t3[:, 0, c, :], rsum3[:, c:c + 1], None, ALU.mult)
                    last.then_inc(p3_ready, 1)
                if f:
                    normalise(0)
                moments_dve(2, at)
                if f:
                    normalise(1)
                if m:
                    elu_head(0)
                if e:
                    dve.wait_ge(y_norm, ge * 2 + 2)
                    for c in range(G):
                        last = nc.vector.tensor_scalar(y[:, c, :], y[:, c, :], mv_y[:, c, 0:1], rstd_y[:, c:c + 1],
                                                       ALU.subtract, ALU.mult)
                    last.then_inc(yn_ready, 1)
                if m:
                    elu_head(1)
                    low_head(0, gm)
                    low_head(1, gm)
                    elu_head(2)
                if l:
                    dve.wait_ge(at3_exp, gl + 1)
                    nc.vector.tensor_scalar(em3[:, :, :, :], em3[:, :, :, :], 1.0, -1.0, ALU.min, ALU.add).then_inc(at3_elu, 1)
                    dve.wait_ge(at3_elu, gl * 2 + 1)
                    if positive(gl):
                        dve.wait_ge(y_full, gl)
                    nc.vector.tensor_tensor(outT[:, :, :, :], bank[7][:, :].rearrange("p (k c n) -> p k c n", k=KC, c=G),
                                            em3[:, :, :, :], ALU.max).then_inc(at3_elu, 1)
                if o2:
                    dve.wait_ge(wo2_full, go * 4 + 4)
                    if positive(go - 1):
                        dve.wait_ge(at3_full, go - 1)
                    nc.vector.tensor_copy(wh2[:, po, 1, :], bank[6][:, 0:D + 2]).then_inc(wh2_dve, 1)
                    dve.wait_ge(wh2_dve, go + 1)
                    dve.wait_ge(wh2_act, go + 1)
                    if positive(go):
                        dve.wait_ge(s3_full, go)
                    for c in range(G):
                        last = nc.vector.tensor_scalar(diag[:, 0, c, :], ident, wh2[:, po, c, D + 1:D + 2], None, ALU.mult)
                    last.then_inc(diag2, 1)
                if m:
                    elu_head(3)
                    low_head(2, gm)
                if isinstance(at.t, int) and at.t == 0:
                    for i, (lo, w, hi) in enumerate(((wh_lo, wh, wh_hi), (wout_lo, wout, wout_hi))):
                        dve.wait_ge(w_hi, i + 1)
                        nc.vector.tensor_tensor(flat(lo), flat(w), flat(hi).bitcast(FP32), ALU.subtract).then_inc(w_lo, 1)

            if PHASES > 2:
                dve.wait_ge(pre[1].x, NG)
                run_steps(dve, NG, step2, deepest=4)

            def step3(at):
                n, gn, _ = at.group(-1)
                f, g, p = at.group(0)
                m, gm, pm = at.group(1)
                e, ge, pe_ = at.group(3)
                pre_dve(dve, 3, at)
                if e:
                    dve.wait_ge(at4_full, ge + 1)
                    if positive(ge):
                        dve.wait_ge(pre[3].x, ge)
                    nc.vector.reciprocal(rsum3[:, :], sum3[:, pe_, :]).then_inc(rsum4, 1)
                if m:
                    xs = x_all[:, bass.ds(gm * G, G), F3:D]
                    nc.vector.tensor_tensor(xs, xs, h3[:, at.quarter(1), :, 0:F3], ALU.add)
                stats_written(dve, 3, at)
                if e:
                    dve.wait_ge(rsum4, ge + 1)
                    for c in range(G):
                        xs = x_all[:, bass.ds(ge * G + c, 1), 0:F3].rearrange("p a d -> p (a d)")
                        last = nc.vector.scalar_tensor_tensor(xs, bank[4][:, c * F3:(c + 1) * F3], rsum3[:, c:c + 1], xs, ALU.mult, ALU.add)
                    last.then_inc(pre[3].x, 1)
                moments_dve(3, at)
                if m:
                    dve.wait_ge(scores4, gm + 1)
                    nc.vector.scalar_tensor_tensor(t3[:, pm], t3[:, pm], LEAK3, t3[:, pm], ALU.mult, ALU.max).then_inc(soft4, 1)
                    dve.wait_ge(soft4, gm * 3 + 1)
                    nc.vector.tensor_tensor(t3[:, pm], t3[:, pm], neg3[:, :].unsqueeze(1).broadcast_to([N, G, N]), ALU.add).then_inc(soft4, 1)
                if f:
                    dve.wait_ge(h3_ready, g + 1)
                    if positive(g - 1):
                        dve.wait_ge(s4_full, g - 1)
                    for c in range(G):
                        last = nc.vector.tensor_scalar(diag[:, p, c, :], ident, h3[:, at.quarter(0), c, F3 + 1:F3 + 2], None, ALU.mult)
                    last.then_inc(diag3, 1)
                if m:
                    dve.wait_ge(soft4, gm * 3 + 2)
                    nc.vector.tensor_reduce(negtop[:, :], t3[:, pm], AX.X, ALU.max, negate=True).then_inc(soft4, 1)
                if n:
                    dve.wait_ge(hT3_full, gn + 1)
                    if positive(gn):
                        dve.wait_ge(w3_full, gn)
                    nc.vector.tensor_copy(hT[:, :, :, :], bank[0][:, :].rearrange("p (k c n) -> p k c n", k=KC, c=G)).then_inc(hT3, 1)

            if PHASES > 3:
                dve.wait_ge(pre[2].x, NG)
                run_steps(dve, NG, step3, 4)

        @block.scalar
        def _(act):
            def step0(at):
                f, g, p = at.group(0)
                b, gb, pb = at.group(1)

                def probs_T(r):
                    act.wait_ge(pT0_full, gb * 4 + r + 1)
                    if positive(gb) and r == 0:
                        act.wait_ge(av_full, gb * 2)
                    nc.scalar.copy(probsT[:, r], bank[2][:, :].rearrange("p (k n) -> p k n", k=4)).then_inc(pT0_act, 1)

                def exp(u, g):
                    act.wait_ge(s0_sub, g * 2 + u + 1)
                    nc.scalar.activation(probs[:, 2 * u:2 * u + 2], probs[:, 2 * u:2 * u + 2], ACT.Exp,
                                         scale=float(DH) ** -0.5).then_inc(p0_ready, 1)

                n, gn, _ = at.group(-1)
                if n and positive(gn - 1):
                    act.wait_ge(hT0_full, gn - 1)
                pre_act(act, 0, at)
                if f:
                    act.wait_ge(q_full, g + 1)
                    if positive(g):
                        act.wait_ge(s0_full, g * 4)
                    for c in range(KC):
                        last = nc.scalar.activation(qT[:, c], bank[1][:, c * 256:(c + 1) * 256].rearrange("p (c n) -> p c n", c=G),
                                                    ACT.Identity, bias=bq_c[:, c:c + 1])
                    last.then_inc(q_ready, 1)
                if b:
                    exp(1, gb)
                    probs_T(0)
                    probs_T(2)
                if f:
                    act.wait_ge(v_full, g + 1)
                    if positive(g - 1):
                        act.wait_ge(av_full, (g - 1) * 2)
                    nc.scalar.copy(v1[:, p, :, :, 0:DH].rearrange("p c h e -> p (c h) e"),
                                   bank[1][:, :].rearrange("p (k e) -> p k e", e=DH)).then_inc(v_ready, 1)
                n, gn, _ = at.group(-1)
                if n:
                    act.wait_ge(hT0_full, gn + 1)
                    if positive(gn):
                        act.wait_ge(v_full, gn)
                    nc.scalar.copy(hT_hi[:, :, :, :], bank[0][:, :].rearrange("p (k c n) -> p k c n", k=KC, c=G)).then_inc(hT0_hi, 1)
                if b:
                    act.wait_ge(aT_full, gb + 1)
                    if positive(gb):
                        act.wait_ge(o_full, gb)
                    nc.scalar.copy(att0T[:, :, :, :], bank[2][:, :].rearrange("p (k c n) -> p k c n", k=KC, c=G)).then_inc(aT_ready, 1)
                if f:
                    exp(0, g)

            act.wait_ge(pool_setup, 1)
            act.wait_ge(loads_done, LOADED)
            for i, dst in ((0, wqT_hi), (2, wvT_hi)):
                act.wait_ge(weights_T, i + 1)
                nc.scalar.copy(dst[:, :, :], bank[i][:, :].rearrange("p (c o) -> p c o", c=2)).then_inc(weights_act, 1)
            run_steps(act, NG, step0)

            def step1(at):
                f, g, p = at.group(0)
                if f:
                    act.wait_ge(hdT_full, g + 1)
                    if positive(g - 1):
                        act.wait_ge(o1_full, g - 1)
                    nc.scalar.copy(hdT_hi[:, p], bank[p][:, :].rearrange("p (k c n) -> p k c n", k=KC, c=G)).then_inc(hdT_ready[0], 1)
                    act.wait_ge(ahT_full, g + 1)
                    nc.scalar.copy(ahT_hi[:, p], bank[2 + p][:, :].rearrange("p (k c n) -> p k c n", k=KC, c=G)).then_inc(ahT_ready[0], 1)
                n, gn, _ = at.group(-1)
                if n and positive(gn - 1):
                    act.wait_ge(ahT_full, gn - 1)
                pre_act(act, 1, at)

            if PHASES > 1:
                act.wait_ge(pre[0].x, NG)
                act.wait_ge(weights_T, 6)
                nc.scalar.copy(adjT[:, :], bank[6][:, 0:N]).then_inc(weights_act, 1)
                for i in range(2):
                    act.wait_ge(weights_T, 7 + i)
                    nc.scalar.copy(w1T_hi[:, i * 2:i * 2 + 2, :], bank[4 + i][:, :].rearrange("p (c o) -> p c o", c=2)).then_inc(weights_act, 1)
                run_steps(act, NG, step1)

            def step2(at):
                f, g, p = at.group(0)
                m, gm, pm = at.group(1)
                o2, go, po = at.group(2)
                l, gl, pl = at.group(3)

                def high_agg(i):
                    act.wait_ge(agg_full, gm * 4 + i + 1)
                    if positive(gm) and i == 0:
                        act.wait_ge(hd2_full, gm * 4)
                    c, dc = i // 2, i % 2
                    nc.scalar.copy(aggT_hi[:, dc, :, c, :], bank[3 + (2 + i) % 4][:, :].rearrange("p (h n) -> p h n", h=H2)).then_inc(agg_hi, 1)

                def exp_head(i):
                    act.wait_ge(hd2_full, gm * 4 + i + 1)
                    if i >= 2 or positive(gm):
                        act.wait_ge(hd2_lo, gm * 4 + i - 1)
                    nc.scalar.activation(em[:, i % 2], bank[3 + i % 2][:, :].rearrange("p (k n) -> p k n", k=KC),
                                         ACT.Exp).then_inc(hd2_exp, 1)

                def high_head(i, gm):
                    act.wait_ge(hd2_elu, gm * 8 + 2 * i + 2)
                    if positive(gm):
                        act.wait_ge(wo2_full, gm * 4 - 3 + i)
                    nc.scalar.copy(headsT_hi[:, i].rearrange("p k c n -> p k (c n)"), em[:, i % 2]).then_inc(hd2_hi, 1)

                def scores_out(c):
                    act.wait_ge(s2_full, g * 2 + c + 1)
                    if positive(g) and c == 0:
                        act.wait_ge(pT2_full, g * 2)
                    nc.scalar.activation(probs[:, c], bank[1 + c][:, :].rearrange("p (h n) -> p h n", h=H2),
                                         ACT.Identity).then_inc(scores2, 1)

                def exp_scores(c):
                    act.wait_ge(soft2, g * 4 + c * 2 + 2)
                    for hh in range(H2):
                        last = nc.scalar.activation(probs[:, c, hh, :], probs[:, c, hh, :], ACT.Exp, bias=negtop2[:, c, hh:hh + 1],
                                                    accum_out=sum2[:, c, hh:hh + 1])
                    last.then_inc(exp2, 1)

                def probs_T(c):
                    act.wait_ge(pT2_full, gm * 2 + c + 1)
                    if positive(gm) and c == 0:
                        act.wait_ge(agg_full, gm * 4)
                    nc.scalar.copy(probsT[:, c], bank[3 + c][:, :].rearrange("p (h n) -> p h n", h=H2)).then_inc(pT2_ready, 1)

                if m:
                    probs_T(0)
                if o2:
                    high_head(3, go)
                if m:
                    probs_T(1)
                    if not positive(gm):
                        act.wait_ge(w_lo, 2)
                    high_agg(0)
                    high_agg(1)
                if f:
                    scores_out(0)
                if m:
                    high_agg(2)
                if f:
                    scores_out(1)
                if m:
                    high_agg(3)
                if l:
                    act.wait_ge(s3_full, gl + 1)
                    act.wait_ge(wh2_dve, gl + 1)
                    act.wait_ge(wh2_act, gl + 1)
                    if positive(gl):
                        act.wait_ge(pT3_full, gl)
                    for c in range(G):
                        last = nc.scalar.activation(t3[:, 0, c, :], bank[7][:, c * N:(c + 1) * N], ACT.Identity,
                                                    bias=wh2[:, pl, c, D:D + 1])
                    last.then_inc(scores3, 1)
                if f:
                    exp_scores(0)
                if l:
                    act.wait_ge(top3, gl * 2 + 2)
                    for c in range(G):
                        last = nc.scalar.activation(t3[:, 0, c, :], t3[:, 0, c, :], ACT.Exp, bias=negtop[:, c:c + 1],
                                                    accum_out=sum3[:, 0, c:c + 1])
                    last.then_inc(exp3, 1)
                if f:
                    exp_scores(1)
                if m:
                    exp_head(0)
                    exp_head(1)
                    high_head(0, gm)
                if l:
                    act.wait_ge(pT3_full, gl + 1)
                    if positive(gl):
                        act.wait_ge(at3_full, gl)
                    nc.scalar.copy(p3T[:, :, :], bank[7][:, 0:G * N].rearrange("p (c n) -> p c n", c=G)).then_inc(pT3_ready, 1)
                if m:
                    high_head(1, gm)
                    exp_head(2)
                if l:
                    act.wait_ge(at3_full, gl + 1)
                    if positive(gl):
                        act.wait_ge(at3_elu, gl * 2)
                    nc.scalar.activation(em3[:, :, :, :], bank[7][:, :].rearrange("p (k c n) -> p k c n", k=KC, c=G),
                                         ACT.Exp).then_inc(at3_exp, 1)
                if o2:
                    act.wait_ge(wo2_full, go * 4 + 4)
                    if positive(go - 1):
                        act.wait_ge(at3_full, go - 1)
                    nc.scalar.copy(wh2[:, po, 0, :], bank[5][:, 0:D + 2]).then_inc(wh2_act, 1)
                n, gn, _ = at.group(-1)
                if n and positive(gn - 1):
                    act.wait_ge(agg_full, (gn - 1) * 4)
                pre_act(act, 2, at)
                if n and not positive(gn):
                    act.wait_ge(late_setup, LATE_DONE)
                    for hi, w in ((wh_hi, wh), (wout_hi, wout)):
                        nc.scalar.copy(flat(hi), flat(w)).then_inc(w_hi, 1)
                if m:
                    exp_head(3)
                    high_head(2, gm)
                if l:
                    act.wait_ge(u_full, gl + 1)
                    if positive(gl):
                        act.wait_ge(y_full, gl)
                    for c in range(KC):
                        last = nc.scalar.activation(uT[:, c], bank[7][:, c * 256:(c + 1) * 256].rearrange("p (c n) -> p c n", c=G),
                                                    ACT.Relu, bias=b1_c[:, c:c + 1])
                    last.then_inc(u_ready, 1)

            if PHASES > 2:
                act.wait_ge(pre[1].x, NG)
                run_steps(act, NG, step2, deepest=4)

            def step3(at):
                f, g, p = at.group(0)
                m, gm, pm = at.group(1)
                l, gl, pl = at.group(2)
                if m:
                    act.wait_ge(s4_full, gm + 1)
                    if positive(gm - 1):
                        act.wait_ge(pT4_full, gm - 1)
                    for c in range(G):
                        last = nc.scalar.activation(t3[:, pm, c, :], bank[2][:, c * N:(c + 1) * N], ACT.Identity,
                                                    bias=h3[:, at.quarter(1), c, F3:F3 + 1])
                    last.then_inc(scores4, 1)
                if l:
                    act.wait_ge(pT4_full, gl + 1)
                    if positive(gl):
                        act.wait_ge(at4_full, gl)
                    nc.scalar.copy(p3T[:, :, :], bank[3][:, 0:G * N].rearrange("p (c n) -> p c n", c=G)).then_inc(pT4_ready, 1)
                if f:
                    act.wait_ge(w3_full, g + 1)
                    if positive(g - 3):
                        act.wait_ge(at4_full, g - 3)
                    nc.scalar.copy(h3[:, at.quarter(0)], bank[1][:, 0:G * (F3 + 2)].rearrange("p (c d) -> p c d", c=G)).then_inc(h3_ready, 1)
                n, gn, _ = at.group(-1)
                if n and positive(gn - 1):
                    act.wait_ge(hT3_full, gn - 1)
                pre_act(act, 3, at)
                if m:
                    act.wait_ge(soft4, gm * 3 + 3)
                    if positive(gm - 1):
                        act.wait_ge(rsum4, gm - 1)
                    for c in range(G):
                        last = nc.scalar.activation(t3[:, pm, c, :], t3[:, pm, c, :], ACT.Exp, bias=negtop[:, c:c + 1],
                                                    accum_out=sum3[:, pm, c:c + 1])
                    last.then_inc(exp4, 1)

            if PHASES > 3:
                act.wait_ge(pre[2].x, NG)
                run_steps(act, NG, step3, 4)

        @block.tensor
        def _(pe):
            pe.wait_ge(loads_done, LOADED)
            for i in range(4):
                for k in range(KC):
                    for c in range(KC):
                        last = nc.tensor.transpose(bank[i][:, (k * KC + c) * N:(k * KC + c + 1) * N], raw[:, i, c, k * N:(k + 1) * N], ident)
                last.then_inc(weights_T, 1)
            pe.wait_ge(dve_setup, BV_DONE)
            pe.wait_ge(weights_dve, 2)
            for k in range(KC):
                last = nc.tensor.matmul(bank[7][:, 0:D], bv_wide[:, k, :], woT[:, k, :], start=(k == 0), stop=(k == KC - 1))
            last.then_inc(weights_T, 1)
            pe.wait_ge(weights_dve, 5)
            pe.wait_ge(dve_setup, BO_DONE)

            def transpose_group(dst, src):
                for k in range(KC):
                    for c in range(G):
                        last = nc.tensor.transpose(dst[:, (k * G + c) * N:(k * G + c + 1) * N], src[:, c, k * N:(k + 1) * N], ident)
                return last

            def step0(at):
                f, g, p = at.group(0)
                b, gb, pb = at.group(1)

                def project_T(dst, w_hi, w_lo):
                    for o in range(KC):
                        for k in range(KC):
                            for w, src in ((w_hi, hT_hi), (w_lo, hT_hi), (w_hi, hT_lo)):
                                last = nc.tensor.matmul(dst[:, o * G * N:(o + 1) * G * N], w[:, k, o * N:(o + 1) * N],
                                                        src[:, k].rearrange("p c n -> p (c n)"),
                                                        start=(k == 0 and w is w_hi and src is hT_hi), stop=(k == KC - 1 and src is hT_lo))
                    return last

                def values(c):
                    for k in range(KC):
                        for src, w in ((hT_hi, wvT_hi), (hT_hi, wvT_lo), (hT_lo, wvT_hi)):
                            last = nc.tensor.matmul(bank[1][:, c * D:(c + 1) * D], src[:, k, c, :], w[:, k, :],
                                                    start=(k == 0 and src is hT_hi and w is wvT_hi), stop=(k == KC - 1 and src is hT_lo))
                    return last

                def probs_T(r, first):
                    pe.wait_ge(p0_ready, gb * 2 + r // 2 + 1)
                    if first is not None:
                        pe.wait_ge(*first)
                    for k in range(4):
                        last = nc.tensor.transpose(bank[2 + r % 2][:, k * N:(k + 1) * N], probs[:, r, k, :], ident)
                    last.then_inc(pT0_full, 1)

                if f:
                    pe.wait_ge(hT0_lo, g + 1)
                    if positive(g):
                        pe.wait_ge(v_ready, g)
                    project_T(bank[1], wqT_hi, wqT_lo).then_inc(q_full, 1)
                if b:
                    probs_T(0, (aT_ready, gb) if positive(gb) else None)
                    probs_T(1, (pre[0].x, gb) if positive(gb) else None)
                if f:
                    project_T(bank[0], wkT_hi, wkT_lo).then_inc(k_full, 1)
                    pe.wait_ge(q_ready, g + 1)
                    values(0)
                if b:
                    probs_T(2, (pT0_act, gb * 2 + 1))
                    probs_T(3, (pT0_dve, gb * 2 + 1))
                if f:
                    values(1).then_inc(v_full, 1)
                if b:
                    pe.wait_ge(v_ready, gb + 1)
                def attend(i):
                    c, hh = i // H0, i % H0
                    ins = nc.tensor.matmul(bank[2 + c][:, hh * (DH + 1):(hh + 1) * (DH + 1)],
                                           probsT[:, hh % 4, (hh // 4) * G + c, :], v1[:, pb, c, hh, :], start=True, stop=True)
                    if hh == H0 - 1:
                        ins.then_inc(av_full, 1)

                n, gn, pn = at.group(-1)
                if n:
                    pe.wait_ge(pre[0].h, gn + 1)
                    if positive(gn):
                        pe.wait_ge(k_ready, gn)
                    transpose_group(bank[0], h[:, pn]).then_inc(hT0_full, 1)
                if f:
                    pe.wait_ge(k_ready, g + 1)
                    if positive(g):
                        pe.wait_ge(s0_sub, g * 2)
                if b:
                    pe.wait_ge(pT0_act, gb * 2 + 2)
                    pe.wait_ge(pT0_dve, gb * 2 + 2)
                for i in range(4):
                    if b:
                        for u in range(2):
                            attend(i * 4 + u)
                    if f:
                        nc.tensor.matmul(bank[4 + i][:, :], ident_bf[:, :], hide0[:, :, :], start=True, stop=False)
                    if b:
                        for u in range(2, 4):
                            attend(i * 4 + u)

                def scores(k):
                    for c in range(G):
                        for r in range(4):
                            i = k * G + c
                            rows = slice(r * DH, (r + 1) * DH)
                            last = nc.tensor.matmul(bank[4 + r][:, i * N:(i + 1) * N], qT[rows, k, c, :], kT[rows, k, c, :],
                                                    start=False, stop=(i == KC * G - 1))
                            if i == KC * G - 1:
                                last.then_inc(s0_full, 1)

                if f:
                    scores(0)
                if b:
                    pe.wait_ge(att0_ready, gb + 1)
                    transpose_group(bank[2], att0[:, :].rearrange("p c h e -> p c (h e)")).then_inc(aT_full, 1)
                if f:
                    scores(1)
                if b:
                    pe.wait_ge(aT_ready, gb + 1)
                    for c in range(G):
                        for k in range(KC):
                            last = nc.tensor.matmul(bank[3][:, c * D:(c + 1) * D], att0T[:, k, c, :], woT[:, k, :],
                                                    start=(k == 0), stop=(k == KC - 1))
                    last.then_inc(o_full, 1)

            run_steps(pe, NG, step0)

            def step1(at):
                f, g, p = at.group(0)
                b, gb, pb = at.group(1)
                if f:
                    pe.wait_ge(hd_ready, g + 1)
                    if positive(g - 1):
                        pe.wait_ge(hdT_ready[1], g - 1)
                    transpose_group(bank[p], hd[:, p]).then_inc(hdT_full, 1)
                    if positive(g - 1):
                        pe.wait_ge(ahT_ready[1], g - 1)
                    for k in range(KC):
                        for c in range(G):
                            last = nc.tensor.matmul(bank[2 + p][:, (k * G + c) * N:(k * G + c + 1) * N], h[:, p, c, k * N:(k + 1) * N],
                                                    adjT[:, :], start=True, stop=True)
                    last.then_inc(ahT_full, 1)
                if b:
                    pe.wait_ge(hdT_ready[1], gb + 1)
                    pe.wait_ge(ahT_ready[1], gb + 1)
                    if positive(gb - 1):
                        pe.wait_ge(pre[1].x, gb - 1)
                    for c in range(G):
                        for k in range(2 * KC):
                            src_hi, src_lo = (src[:, pb, k % KC, c, :] for src in ((hdT_hi, hdT_lo) if k < KC else (ahT_hi, ahT_lo)))
                            o = bank[4 + pb][:, c * D:(c + 1) * D]
                            nc.tensor.matmul(o, src_hi, w1T_hi[:, k, :], start=(k == 0), stop=False)
                            nc.tensor.matmul(o, src_hi, w1T_lo[:, k, :], start=False, stop=False)
                            last = nc.tensor.matmul(o, src_lo, w1T_hi[:, k, :], start=False, stop=(k == 2 * KC - 1))
                    last.then_inc(o1_full, 1)

            if PHASES > 1:
                pe.wait_ge(pre[0].x, NG)
                pe.wait_ge(later_loads_done, LATER_LOADED)
                nc.tensor.transpose(bank[6][:, 0:N], adj_f[:, :], ident).then_inc(weights_T, 1)
                for i in range(2):
                    for k in range(KC):
                        for c in range(KC):
                            last = nc.tensor.transpose(bank[4 + i][:, (k * KC + c) * N:(k * KC + c + 1) * N],
                                                       raw1[:, c, (i * KC + k) * N:(i * KC + k + 1) * N], ident)
                    last.then_inc(weights_T, 1)
                pe.wait_ge(weights_act, 5)
                pe.wait_ge(w1_lo, 2)
                run_steps(pe, NG, step1)

            def step2(at):
                f, g, p = at.group(0)
                m, gm, pm = at.group(1)
                o2, go, po = at.group(2)
                l, gl, pl = at.group(3)
                e, ge, pe_ = at.group(4)

                def agg(i):
                    c, dc = i // 2, i % 2
                    if dc == 0:
                        pe.wait_ge(pT2_ready, gm * 2 + c + 1)
                    if i < 2 and positive(gm - 1):
                        pe.wait_ge((wh2_act, wh2_dve)[i], gm - 1)
                    nc.tensor.matmul(bank[3 + (2 + i) % 4][:, :], h[:, pm, c, dc * N:(dc + 1) * N],
                                     probsT[:, c].rearrange("p h n -> p (h n)"), start=True, stop=True).then_inc(agg_full, 1)

                def head(i):
                    for o in range(KC):
                        for k in range(KC):
                            for w, src in ((wh_hi, aggT_hi), (wh_lo, aggT_hi), (wh_hi, aggT_lo)):
                                last = nc.tensor.matmul(bank[3 + i % 2][:, o * G * N:(o + 1) * G * N], w[:, k, i, o * N:(o + 1) * N],
                                                        src[:, k, i].rearrange("p c n -> p (c n)"), start=(k == 0 and w is wh_hi and src is aggT_hi),
                                                        stop=(k == KC - 1 and src is aggT_lo))
                    last.then_inc(hd2_full, 1)

                def out_product(i):
                    pe.wait_ge(hd2_lo, go * 4 + i + 1)
                    for c in range(G):
                        if i == 0 and m:
                            pe.wait_ge(agg_lo, gm * 4 + 1 + c)
                        for o in range(KC):
                            k = i * KC + o
                            for src, w in ((headsT_hi, wout_hi), (headsT_hi, wout_lo), (headsT_lo, wout_hi)):
                                last = nc.tensor.matmul(bank[5 + c][:, 0:D + 2], src[:, i, o, c, :], w[:, k, :],
                                                        start=(k == 0 and src is headsT_hi and w is wout_hi),
                                                        stop=(k == H2 * KC - 1 and src is headsT_lo))
                    last.then_inc(wo2_full, 1)

                if f:
                    pe.wait_ge(pre[2].h, g + 1)
                    if positive(g):
                        pe.wait_ge(lr_step, g * 2)
                    transpose_group(bank[0], h[:, p]).then_inc(hT2_full, 1)
                if m:
                    for c in range(G):
                        pe.wait_ge(soft2n, gm * 4 + c * 2 + 2)
                        if positive(gm):
                            pe.wait_ge(hd2_elu, gm * 8 - 2 + 2 * c)
                        for hh in range(H2):
                            last = nc.tensor.transpose(bank[3 + c][:, hh * N:(hh + 1) * N], probs[:, c, hh, :], ident)
                        last.then_inc(pT2_full, 1)
                if f:
                    pe.wait_ge(hT2, g + 1)
                    for c in range(G):
                        for k in range(KC):
                            last = nc.tensor.matmul(bank[0][c * 32:(c + 1) * 32, 0:N], wh_f[:, k, :], hT[:, k, c, :],
                                                    start=(k == 0), stop=(k == KC - 1))
                    last.then_inc(f_full, 1)
                if m:
                    agg(0)
                if e:
                    pe.wait_ge(u_ready, ge + 1)
                    for c in range(G):
                        for k in range(KC):
                            nc.tensor.matmul(bank[7][:, c * D:(c + 1) * D], uT[:, k, c, :], ffn2[:, k, :], start=(k == 0), stop=False)
                        for k in range(KC):
                            last = nc.tensor.matmul(bank[7][:, c * D + k * N:c * D + (k + 1) * N], outT[:, k, c, :], ident,
                                                    start=False, stop=(k == KC - 1))
                    last.then_inc(y_full, 1)
                if m:
                    agg(1)
                if f:
                    pe.wait_ge(lr_step, g * 2 + 2)
                    if positive(g):
                        pe.wait_ge(scores2, g * 2)
                    for c in range(G):
                        nc.tensor.matmul(bank[1 + c][:, :], ident_bf[:, :], hide2[:, :, :], start=True, stop=False)
                    for c in range(G):
                        rows = slice(c * 32, (c + 1) * 32)
                        nc.tensor.matmul(bank[1 + c][:, :], left[rows, :], right[rows].rearrange("p h n -> p (h n)"),
                                         start=False, stop=True).then_inc(s2_full, 1)
                if m:
                    agg(2)
                    agg(3)
                if l:
                    pe.wait_ge(diag2, gl + 1)
                    if positive(gl):
                        pe.wait_ge(y_step, gl * 3 - 2)
                    nc.tensor.matmul(bank[7][:, 0:G * N], ident_bf[:, :], hide2[:, 0:G, :], start=True, stop=False)
                    nc.tensor.matmul(bank[7][:, 0:G * N], ones[:, :], diag[:, 0].rearrange("p c n -> p (c n)"),
                                     start=False, stop=True).then_inc(s3_full, 1)
                if o2:
                    out_product(0)
                    out_product(1)
                if m:
                    if not positive(gm):
                        pe.wait_ge(w_lo, 2)
                    pe.wait_ge(agg_lo, gm * 4 + 4)
                    head(0)
                    head(1)
                if l:
                    pe.wait_ge(p3_ready, gl + 1)
                    for c in range(G):
                        last = nc.tensor.transpose(bank[7][:, c * N:(c + 1) * N], t3[:, 0, c, :], ident)
                    last.then_inc(pT3_full, 1)
                if o2:
                    out_product(2)
                if m:
                    pe.wait_ge(hd2_elu, gm * 8 + 2)
                    head(2)
                if l:
                    pe.wait_ge(pT3_ready, gl + 1)
                    for o in range(KC):
                        for c in range(G):
                            last = nc.tensor.matmul(bank[7][:, (o * G + c) * N:(o * G + c + 1) * N], wh2[:, pl, c, o * N:(o + 1) * N],
                                                    p3T[:, c, :], start=True, stop=True)
                    last.then_inc(at3_full, 1)
                if o2:
                    out_product(3)
                if m:
                    pe.wait_ge(hd2_elu, gm * 8 + 4)
                    head(3)
                if l:
                    pe.wait_ge(at3_elu, gl * 2 + 2)
                    for o in range(KC):
                        for k in range(KC):
                            last = nc.tensor.matmul(bank[7][:, o * G * N:(o + 1) * G * N], ffn1[:, k, o * N:(o + 1) * N],
                                                    outT[:, k].rearrange("p c n -> p (c n)"), start=(k == 0), stop=(k == KC - 1))
                    last.then_inc(u_full, 1)

            if PHASES > 2:
                pe.wait_ge(pre[1].x, NG)
                pe.wait_ge(late_setup, LATE_DONE)
                run_steps(pe, NG, step2, deepest=4)

            def step3(at):
                n, gn, pn = at.group(-1)
                f, g, p = at.group(0)
                m, gm, pm = at.group(1)
                l, gl, pl = at.group(2)
                if m:
                    pe.wait_ge(diag3, gm + 1)
                    if positive(gm):
                        pe.wait_ge(scores4, gm)
                    nc.tensor.matmul(bank[2][:, 0:G * N], ones[:, :], diag[:, pm].rearrange("p c n -> p (c n)"),
                                     start=True, stop=True).then_inc(s4_full, 1)
                if l:
                    pe.wait_ge(exp4, gl + 1)
                    if positive(gl):
                        pe.wait_ge(pT4_ready, gl)
                    for c in range(G):
                        last = nc.tensor.transpose(bank[3][:, c * N:(c + 1) * N], t3[:, pl, c, :], ident)
                    last.then_inc(pT4_full, 1)
                if f:
                    pe.wait_ge(hT3, g + 1)
                    if positive(g):
                        pe.wait_ge(h3_ready, g)
                    for c in range(G):
                        for k in range(KC):
                            last = nc.tensor.matmul(bank[1][:, c * (F3 + 2):(c + 1) * (F3 + 2)], hT[:, k, c, :], w3[:, k, :],
                                                    start=(k == 0), stop=(k == KC - 1))
                    last.then_inc(w3_full, 1)
                if l:
                    pe.wait_ge(pT4_ready, gl + 1)
                    if positive(gl):
                        pe.wait_ge(pre[3].x, gl)
                    for c in range(G):
                        last = nc.tensor.matmul(bank[4][:, c * F3:(c + 1) * F3], p3T[:, c, :], h3[:, at.quarter(2), c, 0:F3], start=True, stop=True)
                    last.then_inc(at4_full, 1)
                if n:
                    pe.wait_ge(pre[3].h, gn + 1)
                    if positive(gn):
                        pe.wait_ge(hT3, gn)
                    transpose_group(bank[0], h[:, pn]).then_inc(hT3_full, 1)

            if PHASES > 3:
                pe.wait_ge(pre[2].x, NG)
                run_steps(pe, NG, step3, 4)


def shape_constants():
    c = np.zeros((N, N + 4 + H2 * N), np.float32)
    c[:, :N] = np.eye(N)
    r = np.arange(N) % 32
    f1, f2 = r < H2, (r >= H2) & (r < 2 * H2)
    c[:, N], c[:, N + 1] = f1, f2
    c[:, N + 2], c[:, N + 3] = f2, f1
    for hh in range(H2):
        c[:, N + 4 + hh * N:N + 4 + (hh + 1) * N] = ((f1 | f2) & (r % H2 == hh))[:, None]
    return c


_INS = ['x', 'adj', 'L0_gnn_Wq', 'L0_gnn_bq', 'L0_gnn_Wk', 'L0_gnn_bk', 'L0_gnn_Wv', 'L0_gnn_bv', 'L0_gnn_Wo', 'L0_gnn_bo',
        'L1_gnn_W', 'L1_gnn_b', 'L2_gnn_W_heads', 'L2_gnn_a_heads', 'L2_gnn_W_out', 'L2_gnn_a_out', 'L2_gnn_w1', 'L2_gnn_b1',
        'L2_gnn_w2', 'L2_gnn_b2', 'L2_gnn_ln_gamma', 'L2_gnn_ln_beta', 'L3_gnn_W', 'L3_gnn_a']


def kernel(**inputs):
    import concourse.bacc as bacc
    from concourse.bass_utils import run_bass_kernel_spmd

    nc = bacc.Bacc("TRN2", target_bir_lowering=False, num_devices=1)
    arrays = {f"in_{name}": np.ascontiguousarray(inputs[name]) for name in _INS}
    for name in ('L0_gnn_bq', 'L0_gnn_bk', 'L0_gnn_bv', 'L2_gnn_b1'):
        arrays[f"in_{name}"] = np.ascontiguousarray(inputs[name].reshape(KC, N).T)
    arrays["in_shape_consts"] = shape_constants()
    args = [nc.dram_tensor(name, a.shape, mybir.dt.from_np(a.dtype), kind="ExternalInput").ap() for name, a in arrays.items()]
    out = nc.dram_tensor("out_x", arrays["in_x"].shape, FP32, kind="ExternalOutput").ap()
    build_program(nc, *args, out)
    return run_bass_kernel_spmd(nc, [arrays], core_ids=[0]).results[0]["out_x"]
```
